# Optimizing a Trainium2 kernel written in Bass

```python
import numpy as np
import jax
import jax.numpy as jnp

def _softmax(x, axis=-1):
    return jax.nn.softmax(x, axis=axis)

def _gelu(x):
    return jax.nn.gelu(x, approximate=True)

def _silu(x):
    return jax.nn.silu(x)

def _sigmoid(x):
    return jax.nn.sigmoid(x)

def _layernorm(x, axis=-1, eps=1e-05):
    m = jnp.mean(x, axis=axis, keepdims=True)
    v = jnp.var(x, axis=axis, keepdims=True)
    return (x - m) / jnp.sqrt(v + eps)

def _scatter_add(tgt, idx, src, axis=0):
    return tgt.at[idx].add(src)

def _segment_sum(src, seg, n):
    return jax.ops.segment_sum(src, seg, n)
kernel_name = 'mk_lm_tower_d4_tok_ids256_r4_a9d2ee'

def setup_inputs(seed: int=0):
    np.random.seed(seed)
    _w = jnp.asarray

    def _rec_inputs():
        import jax
        import jax.numpy as jnp
        _rk = jax.random.key(seed)
        x = jax.random.randint(jax.random.fold_in(_rk, 1), (16, 256), 0, 12564, jnp.int32)
        return x
    x = _rec_inputs()

    def _L0_tok_setup():
        import jax, jax.numpy as jnp
        import numpy as np
        INP_SIZE = 50257
        HIDDEN = 64
        KSIZE = 9
        B, T = (16, 1024)
        key = jax.random.key(seed)
        k1, k2, k3, k4 = jax.random.split(key, 4)
        x = jax.random.randint(k1, (B, T), 0, INP_SIZE, dtype=jnp.int64 if jax.config.jax_enable_x64 else jnp.int32)
        emb = jax.random.normal(k2, (INP_SIZE, HIDDEN), dtype=jnp.float32) * 0.02
        fan_in = HIDDEN * KSIZE
        bound = 1.0 / np.sqrt(fan_in)
        W = jax.random.uniform(k3, (HIDDEN, HIDDEN, KSIZE), dtype=jnp.float32, minval=-bound, maxval=bound)
        b = jax.random.uniform(k4, (HIDDEN,), dtype=jnp.float32, minval=-bound, maxval=bound)
        return {'x': x, 'emb': emb, 'W': W, 'b': b}
    _L0_tok_all = _L0_tok_setup()
    _L0_tok_in = {k: v for k, v in _L0_tok_all.items() if k in ('emb', 'W', 'b')}
    del _L0_tok_all

    def _L0_attn_setup():
        import jax, jax.numpy as jnp
        import numpy as np
        NUM_HEADS = 8
        key = jax.random.key(seed)
        ks = jax.random.split(key, 5)
        B, N, C = (8, 4096, 64)
        x = jax.random.normal(ks[0], (B, N, C), dtype=jnp.float32)
        Wq = jax.random.normal(ks[1], (C, C), dtype=jnp.float32) * 0.02
        Wkv = jax.random.normal(ks[2], (2 * C, C), dtype=jnp.float32) * 0.02
        Wproj = jax.random.normal(ks[3], (C, C), dtype=jnp.float32) * 0.02
        bproj = jnp.zeros((C,), dtype=jnp.float32)
        return {'x': x, 'Wq': Wq, 'Wkv': Wkv, 'Wproj': Wproj, 'bproj': bproj}
    _L0_attn_all = _L0_attn_setup()
    _L0_attn_in = {k: v for k, v in _L0_attn_all.items() if k in ('Wq', 'Wkv', 'Wproj', 'bproj')}
    del _L0_attn_all

    def _L0_ffn_setup():
        import jax, jax.numpy as jnp
        import numpy as np
        B, T, IN_DIM = (64, 64, 64)
        HID, OUT_DIM = (128, 64)
        N_LAYERS, N_EXPERTS, N_SHARED = (2, 16, 1)
        key = jax.random.key(seed)
        ks = jax.random.split(key, 10)
        s = 0.02
        x = jax.random.normal(ks[0], (B, T, IN_DIM), dtype=jnp.float32)
        route_id = jax.random.randint(ks[1], (B,), 0, N_EXPERTS)
        Wi = jax.random.normal(ks[2], (HID, IN_DIM), dtype=jnp.float32) * s
        bi = jnp.zeros((HID,), dtype=jnp.float32)
        Wr = jax.random.normal(ks[3], (N_LAYERS, N_EXPERTS, HID, HID), dtype=jnp.float32) * s
        br = jax.random.normal(ks[4], (N_LAYERS, N_EXPERTS, HID), dtype=jnp.float32) * s
        Ws = jax.random.normal(ks[5], (N_LAYERS, N_SHARED, HID, HID), dtype=jnp.float32) * s
        bs = jax.random.normal(ks[6], (N_LAYERS, N_SHARED, HID), dtype=jnp.float32) * s
        Wo = jax.random.normal(ks[7], (OUT_DIM, HID), dtype=jnp.float32) * s
        bo = jnp.zeros((OUT_DIM,), dtype=jnp.float32)
        return {'x': x, 'route_id': route_id, 'Wi': Wi, 'bi': bi, 'Wr': Wr, 'br': br, 'Ws': Ws, 'bs': bs, 'Wo': Wo, 'bo': bo}
    _L0_ffn_all = _L0_ffn_setup()
    _L0_ffn_in = {k: v for k, v in _L0_ffn_all.items() if k in ('route_id', 'Wi', 'bi', 'Wr', 'br', 'Ws', 'bs', 'Wo', 'bo')}
    del _L0_ffn_all

    def _L1_attn_setup():
        import jax, jax.numpy as jnp
        import numpy as np
        BN_EPS = 1e-05
        key = jax.random.key(seed)
        ks = jax.random.split(key, 12)
        B, N, d_e, d_a = (16, 512, 64, 64)
        s_e = 1.0 / np.sqrt(d_e)
        return {'x': jax.random.normal(ks[0], (B, N, d_e), dtype=jnp.float32), 'Wq': jax.random.uniform(ks[1], (d_e, d_a), jnp.float32, -s_e, s_e), 'bq': jax.random.uniform(ks[2], (d_a,), jnp.float32, -s_e, s_e), 'Wk': jax.random.uniform(ks[3], (d_e, d_a), jnp.float32, -s_e, s_e), 'bk': jax.random.uniform(ks[4], (d_a,), jnp.float32, -s_e, s_e), 'Wv': jax.random.uniform(ks[5], (d_e, d_e), jnp.float32, -s_e, s_e), 'bv': jax.random.uniform(ks[6], (d_e,), jnp.float32, -s_e, s_e), 'Wl': jax.random.uniform(ks[7], (d_e, d_e), jnp.float32, -s_e, s_e), 'bl': jax.random.uniform(ks[8], (d_e,), jnp.float32, -s_e, s_e), 'gamma': jnp.ones((d_e,), jnp.float32), 'beta': jnp.zeros((d_e,), jnp.float32)}
    _L1_attn_all = _L1_attn_setup()
    _L1_attn_in = {k: v for k, v in _L1_attn_all.items() if k in ('Wq', 'bq', 'Wk', 'bk', 'Wv', 'bv', 'Wl', 'bl', 'gamma', 'beta')}
    del _L1_attn_all

    def _L1_ffn_setup():
        import jax, jax.numpy as jnp
        import numpy as np
        E = 8
        K = 2
        D = 64
        H = 128
        DOUT = 64
        EPS = 1e-05
        key = jax.random.key(seed)
        ks = jax.random.split(key, 9)
        s = 0.02
        return {'x': jax.random.normal(ks[0], (4, 2048, D), jnp.float32), 'gamma': 1.0 + 0.05 * jax.random.normal(ks[1], (D,), jnp.float32), 'beta': 0.05 * jax.random.normal(ks[2], (D,), jnp.float32), 'Wr': 0.01 * jax.random.normal(ks[3], (D, E), jnp.float32), 'br': jnp.zeros((E,), jnp.float32), 'W1': s * jax.random.normal(ks[4], (E, D, H), jnp.float32), 'b1': s * jax.random.normal(ks[5], (E, H), jnp.float32), 'W2': s * jax.random.normal(ks[6], (E, H, DOUT), jnp.float32), 'b2': s * jax.random.normal(ks[7], (E, DOUT), jnp.float32)}
    _L1_ffn_all = _L1_ffn_setup()
    _L1_ffn_in = {k: v for k, v in _L1_ffn_all.items() if k in ('gamma', 'beta', 'Wr', 'br', 'W1', 'b1', 'W2', 'b2')}
    del _L1_ffn_all

    def _L2_attn_setup():
        import math
        import jax, jax.numpy as jnp
        import numpy as np
        ROPE_DIMS = 16
        N_WIN = 16

        def rmsnorm(x, w):
            return x * jax.lax.rsqrt(jnp.mean(x * x, axis=-1, keepdims=True) + 1e-08) * w

        def apply_rope(x, negate=False):
            T = x.shape[2]
            x_pass, x_rope = (x[..., :-ROPE_DIMS], x[..., -ROPE_DIMS:])
            t = jnp.arange(T, dtype=x.dtype)
            if negate:
                t = -t
            k = jnp.arange(ROPE_DIMS // 2, dtype=x.dtype)
            theta = 10000.0 ** (-2.0 * k / ROPE_DIMS)
            freqs = t[:, None] * theta[None, :]
            cos, sin = (jnp.cos(freqs), jnp.sin(freqs))
            x1, x2 = (x_rope[..., 0::2], x_rope[..., 1::2])
            rx1 = x1 * cos - x2 * sin
            rx2 = x1 * sin + x2 * cos
            rx = jnp.stack([rx1, rx2], axis=-1).reshape(x_rope.shape)
            return jnp.concatenate([x_pass, rx], axis=-1)
        key = jax.random.key(seed)
        ks = jax.random.split(key, 14)
        B, T, d, c, nh = (4, 512, 64, 64, 4)
        s = 0.02
        return {'H': jax.random.normal(ks[0], (B, T, d), jnp.float32), 'W_Q': jax.random.normal(ks[1], (nh * c, d), jnp.float32) * s, 'W_K': jax.random.normal(ks[2], (c, d), jnp.float32) * s, 'W_V': jax.random.normal(ks[3], (c, d), jnp.float32) * s, 'wq': 1.0 + 0.1 * jax.random.normal(ks[4], (nh, c), jnp.float32), 'wk': 1.0 + 0.1 * jax.random.normal(ks[5], (c,), jnp.float32), 'wv': 1.0 + 0.1 * jax.random.normal(ks[6], (c,), jnp.float32), 'Wg0': jax.random.normal(ks[7], (64, 2 * c), jnp.float32) * s, 'bg0': jnp.zeros((64,), jnp.float32), 'Wg1': jax.random.normal(ks[8], (64, 2 * c), jnp.float32) * s, 'bg1': jnp.zeros((64,), jnp.float32), 'Wout': jax.random.normal(ks[9], (d, 128), jnp.float32) * s, 'bout': jnp.zeros((d,), jnp.float32)}
    _L2_attn_all = _L2_attn_setup()
    _L2_attn_in = {k: v for k, v in _L2_attn_all.items() if k in ('W_Q', 'W_K', 'W_V', 'wq', 'wk', 'wv', 'Wg0', 'bg0', 'Wg1', 'bg1', 'Wout', 'bout')}
    del _L2_attn_all

    def _L2_ffn_setup():
        import jax, jax.numpy as jnp
        import numpy as np
        NUM_EXPERTS = 8
        TOP_K = 2
        B, S, D = (8, 2048, 64)

        def _moe(tokens, router_w, w1, b1, w2, b2):
            N = tokens.shape[0]
            E = router_w.shape[0]
            logits = tokens.astype(jnp.float32) @ router_w.astype(jnp.float32).T
            probs = jax.nn.softmax(logits, axis=-1)
            rw, re = jax.lax.top_k(probs, TOP_K)
            if TOP_K > 1:
                rw = rw / jnp.maximum(rw.sum(-1, keepdims=True), 1e-12)
            rw = rw.astype(tokens.dtype)
            combine = jnp.zeros((N, E), tokens.dtype).at[jnp.arange(N)[:, None], re].set(rw)
            out = tokens
            for e in range(E):
                h = jax.nn.gelu(tokens @ w1[e] + b1[e], approximate=False)
                y = h @ w2[e] + b2[e]
                out = out + combine[:, e:e + 1] * y
            return out
        key = jax.random.key(seed)
        ks = jax.random.split(key, 4)
        scale = 1.0 / np.sqrt(D).astype(np.float32)
        return {'input_embeddings': jax.random.normal(ks[0], (B, S, D), jnp.float32), 'router_w': jax.random.normal(ks[1], (NUM_EXPERTS, D), jnp.float32) * scale, 'w1': jax.random.normal(ks[2], (NUM_EXPERTS, D, D), jnp.float32) * scale, 'b1': jnp.zeros((NUM_EXPERTS, D), jnp.float32), 'w2': jax.random.normal(ks[3], (NUM_EXPERTS, D, D), jnp.float32) * scale, 'b2': jnp.zeros((NUM_EXPERTS, D), jnp.float32)}
    _L2_ffn_all = _L2_ffn_setup()
    _L2_ffn_in = {k: v for k, v in _L2_ffn_all.items() if k in ('router_w', 'w1', 'b1', 'w2', 'b2')}
    del _L2_ffn_all

    def _L3_attn_setup():
        import jax, jax.numpy as jnp
        import numpy as np
        D_IN, D_OUT, ORDER = (64, 64, 8)
        B, L = (32, 256)
        key = jax.random.key(seed)
        k1, k2, k3, k4 = jax.random.split(key, 4)
        scale = 1.0 / ORDER
        return {'x': jax.random.normal(k1, (B, L, D_IN), dtype=jnp.float32), 'h0': jax.random.normal(k2, (D_IN, D_OUT, 1), dtype=jnp.float32) * scale, 'numerators': jax.random.normal(k3, (2, D_IN, D_OUT, ORDER), dtype=jnp.float32) * scale, 'denumerator': jax.random.normal(k4, (D_IN, D_OUT, ORDER), dtype=jnp.float32) * scale}
    _L3_attn_all = _L3_attn_setup()
    _L3_attn_in = {k: v for k, v in _L3_attn_all.items() if k in ('h0', 'numerators', 'denumerator')}
    del _L3_attn_all

    def _L3_ffn_setup():
        import jax, jax.numpy as jnp
        import numpy as np
        B, S, D = (8, 1024, 64)
        H = 4 * D
        CAPACITY = 0.5
        key = jax.random.key(seed)
        ks = jax.random.split(key, 6)
        x = jax.random.normal(ks[0], (B, S, D), dtype=jnp.float32)
        attention_mask = jnp.zeros((B, 1, 1, S), dtype=jnp.float32)
        wr = jax.random.normal(ks[1], (D, 1), dtype=jnp.float32) * 0.02
        br = jnp.zeros((1,), dtype=jnp.float32)
        w1 = jax.random.normal(ks[2], (D, H), dtype=jnp.float32) * 0.02
        b1 = jnp.zeros((H,), dtype=jnp.float32)
        w2 = jax.random.normal(ks[3], (H, D), dtype=jnp.float32) * 0.02
        b2 = jnp.zeros((D,), dtype=jnp.float32)
        return {'x': x, 'attention_mask': attention_mask, 'wr': wr, 'br': br, 'w1': w1, 'b1': b1, 'w2': w2, 'b2': b2}
    _L3_ffn_all = _L3_ffn_setup()
    _L3_ffn_in = {k: v for k, v in _L3_ffn_all.items() if k in ('attention_mask', 'wr', 'br', 'w1', 'b1', 'w2', 'b2')}
    del _L3_ffn_all
    return {'x': x, 'L0_tok_emb': _L0_tok_in['emb'], 'L0_tok_W': _L0_tok_in['W'], 'L0_tok_b': _L0_tok_in['b'], 'L0_attn_Wq': _L0_attn_in['Wq'], 'L0_attn_Wkv': _L0_attn_in['Wkv'], 'L0_attn_Wproj': _L0_attn_in['Wproj'], 'L0_attn_bproj': _L0_attn_in['bproj'], 'L0_ffn_route_id': _L0_ffn_in['route_id'], 'L0_ffn_Wi': _L0_ffn_in['Wi'], 'L0_ffn_bi': _L0_ffn_in['bi'], 'L0_ffn_Wr': _L0_ffn_in['Wr'], 'L0_ffn_br': _L0_ffn_in['br'], 'L0_ffn_Ws': _L0_ffn_in['Ws'], 'L0_ffn_bs': _L0_ffn_in['bs'], 'L0_ffn_Wo': _L0_ffn_in['Wo'], 'L0_ffn_bo': _L0_ffn_in['bo'], 'L1_attn_Wq': _L1_attn_in['Wq'], 'L1_attn_bq': _L1_attn_in['bq'], 'L1_attn_Wk': _L1_attn_in['Wk'], 'L1_attn_bk': _L1_attn_in['bk'], 'L1_attn_Wv': _L1_attn_in['Wv'], 'L1_attn_bv': _L1_attn_in['bv'], 'L1_attn_Wl': _L1_attn_in['Wl'], 'L1_attn_bl': _L1_attn_in['bl'], 'L1_attn_gamma': _L1_attn_in['gamma'], 'L1_attn_beta': _L1_attn_in['beta'], 'L1_ffn_gamma': _L1_ffn_in['gamma'], 'L1_ffn_beta': _L1_ffn_in['beta'], 'L1_ffn_Wr': _L1_ffn_in['Wr'], 'L1_ffn_br': _L1_ffn_in['br'], 'L1_ffn_W1': _L1_ffn_in['W1'], 'L1_ffn_b1': _L1_ffn_in['b1'], 'L1_ffn_W2': _L1_ffn_in['W2'], 'L1_ffn_b2': _L1_ffn_in['b2'], 'L2_attn_W_Q': _L2_attn_in['W_Q'], 'L2_attn_W_K': _L2_attn_in['W_K'], 'L2_attn_W_V': _L2_attn_in['W_V'], 'L2_attn_wq': _L2_attn_in['wq'], 'L2_attn_wk': _L2_attn_in['wk'], 'L2_attn_wv': _L2_attn_in['wv'], 'L2_attn_Wg0': _L2_attn_in['Wg0'], 'L2_attn_bg0': _L2_attn_in['bg0'], 'L2_attn_Wg1': _L2_attn_in['Wg1'], 'L2_attn_bg1': _L2_attn_in['bg1'], 'L2_attn_Wout': _L2_attn_in['Wout'], 'L2_attn_bout': _L2_attn_in['bout'], 'L2_ffn_router_w': _L2_ffn_in['router_w'], 'L2_ffn_w1': _L2_ffn_in['w1'], 'L2_ffn_b1': _L2_ffn_in['b1'], 'L2_ffn_w2': _L2_ffn_in['w2'], 'L2_ffn_b2': _L2_ffn_in['b2'], 'L3_attn_h0': _L3_attn_in['h0'], 'L3_attn_numerators': _L3_attn_in['numerators'], 'L3_attn_denumerator': _L3_attn_in['denumerator'], 'L3_ffn_attention_mask': _L3_ffn_in['attention_mask'], 'L3_ffn_wr': _L3_ffn_in['wr'], 'L3_ffn_br': _L3_ffn_in['br'], 'L3_ffn_w1': _L3_ffn_in['w1'], 'L3_ffn_b1': _L3_ffn_in['b1'], 'L3_ffn_w2': _L3_ffn_in['w2'], 'L3_ffn_b2': _L3_ffn_in['b2']}

def reference(x, L0_tok_emb, L0_tok_W, L0_tok_b, L0_attn_Wq, L0_attn_Wkv, L0_attn_Wproj, L0_attn_bproj, L0_ffn_route_id, L0_ffn_Wi, L0_ffn_bi, L0_ffn_Wr, L0_ffn_br, L0_ffn_Ws, L0_ffn_bs, L0_ffn_Wo, L0_ffn_bo, L1_attn_Wq, L1_attn_bq, L1_attn_Wk, L1_attn_bk, L1_attn_Wv, L1_attn_bv, L1_attn_Wl, L1_attn_bl, L1_attn_gamma, L1_attn_beta, L1_ffn_gamma, L1_ffn_beta, L1_ffn_Wr, L1_ffn_br, L1_ffn_W1, L1_ffn_b1, L1_ffn_W2, L1_ffn_b2, L2_attn_W_Q, L2_attn_W_K, L2_attn_W_V, L2_attn_wq, L2_attn_wk, L2_attn_wv, L2_attn_Wg0, L2_attn_bg0, L2_attn_Wg1, L2_attn_bg1, L2_attn_Wout, L2_attn_bout, L2_ffn_router_w, L2_ffn_w1, L2_ffn_b1, L2_ffn_w2, L2_ffn_b2, L3_attn_h0, L3_attn_numerators, L3_attn_denumerator, L3_ffn_attention_mask, L3_ffn_wr, L3_ffn_br, L3_ffn_w1, L3_ffn_b1, L3_ffn_w2, L3_ffn_b2):
    import jax
    import jax.numpy as jnp

    def _L0_tok_ref(x, emb, W, b):
        import jax, jax.numpy as jnp
        import numpy as np
        INP_SIZE = 50257
        HIDDEN = 64
        KSIZE = 9
        B, T = (16, 1024)
        offsets = jnp.arange(-(KSIZE // 2), KSIZE // 2 + 1)
        idx = jnp.clip(x[..., None] + offsets, 0, INP_SIZE - 1)
        gathered = emb[idx]
        out = jnp.einsum('btkh,ohk->bto', gathered, W) + b
        return out

    def _L0_attn_ref(x, Wq, Wkv, Wproj, bproj):
        import jax, jax.numpy as jnp
        import numpy as np
        NUM_HEADS = 8
        B, N, C = x.shape
        h = NUM_HEADS
        d = C // h
        q = jnp.einsum('bnc,oc->bno', x, Wq).reshape(B, N, h, d).transpose(0, 2, 1, 3)
        kv = jnp.einsum('bnc,oc->bno', x, Wkv).reshape(B, N, 2, h, d)
        k = kv[:, :, 0].transpose(0, 2, 1, 3)
        v = kv[:, :, 1].transpose(0, 2, 1, 3)
        q = jax.nn.elu(q) + 1.0
        k = jax.nn.elu(k) + 1.0
        k_sum = k.sum(axis=2)
        D_inv = 1.0 / jnp.maximum(jnp.einsum('bhnd,bhd->bhn', q, k_sum), 1e-06)
        context = jnp.einsum('bhnd,bhne->bhde', k, v)
        attn = jnp.einsum('bhnd,bhde->bhne', q, context) * D_inv[..., None]
        out = attn.transpose(0, 2, 1, 3).reshape(B, N, C)
        out = jnp.einsum('bnc,oc->bno', out, Wproj) + bproj
        return out

    def _L0_ffn_ref(x, route_id, Wi, bi, Wr, br, Ws, bs, Wo, bo):
        import jax, jax.numpy as jnp
        import numpy as np
        B, T, IN_DIM = (64, 64, 64)
        HID, OUT_DIM = (128, 64)
        N_LAYERS, N_EXPERTS, N_SHARED = (2, 16, 1)
        flat = x.reshape(-1, x.shape[-1])
        n_tok = flat.shape[0]
        route = jnp.repeat(route_id, n_tok // route_id.shape[0])
        h = jax.nn.relu(flat @ Wi.T + bi)
        n_layers, n_experts = (Wr.shape[0], Wr.shape[1])
        for l in range(n_layers):
            shared = (jnp.einsum('nd,shd->snh', h, Ws[l]) + bs[l][:, None, :]).mean(axis=0)
            routed = jnp.zeros_like(h)
            for e in range(n_experts):
                ye = h @ Wr[l, e].T + br[l, e]
                routed = routed + jnp.where((route == e)[:, None], ye, 0.0)
            h = jax.nn.relu(shared + routed + h)
        out = h @ Wo.T + bo
        return out.reshape(*x.shape[:-1], out.shape[-1])

    def _L1_attn_ref(x, Wq, bq, Wk, bk, Wv, bv, Wl, bl, gamma, beta):
        import jax, jax.numpy as jnp
        import numpy as np
        BN_EPS = 1e-05
        q = x @ Wq + bq
        k = x @ Wk + bk
        v = x @ Wv + bv
        d_a = q.shape[-1]
        score = jnp.einsum('bnd,bmd->bnm', q, k) / jnp.asarray(d_a, q.dtype)
        score = jax.nn.softmax(score, axis=2)
        attn = jnp.einsum('bnm,bmd->bnd', score, v)
        h = attn @ Wl + bl
        mean = jnp.mean(h, axis=(0, 1))
        var = jnp.mean((h - mean) ** 2, axis=(0, 1))
        y = jax.nn.relu((h - mean) * jax.lax.rsqrt(var + BN_EPS) * gamma + beta)
        return y + x

    def _L1_ffn_ref(x, gamma, beta, Wr, br, W1, b1, W2, b2):
        import jax, jax.numpy as jnp
        import numpy as np
        E = 8
        K = 2
        D = 64
        H = 128
        DOUT = 64
        EPS = 1e-05
        mu = jnp.mean(x, axis=-1, keepdims=True)
        var = jnp.mean(jnp.square(x - mu), axis=-1, keepdims=True)
        xn = (x - mu) * jax.lax.rsqrt(var + EPS) * gamma + beta
        logits = jnp.einsum('bsd,de->bse', xn, Wr) + br
        top_vals, top_idx = jax.lax.top_k(logits, K)
        w = jax.nn.softmax(top_vals, axis=-1)
        w_full = jnp.einsum('bsk,bske->bse', w, jax.nn.one_hot(top_idx, E, dtype=w.dtype))
        y = jnp.zeros(x.shape[:-1] + (DOUT,), x.dtype)
        for e in range(E):
            h = jax.nn.gelu(jnp.einsum('bsd,dh->bsh', xn, W1[e]) + b1[e], approximate=False)
            y_e = jnp.einsum('bsh,hd->bsd', h, W2[e]) + b2[e]
            y = y + y_e * w_full[..., e, None]
        return y

    def _L2_attn_ref(H, W_Q, W_K, W_V, wq, wk, wv, Wg0, bg0, Wg1, bg1, Wout, bout):
        import math
        import jax, jax.numpy as jnp
        import numpy as np
        ROPE_DIMS = 16
        N_WIN = 16

        def rmsnorm(x, w):
            return x * jax.lax.rsqrt(jnp.mean(x * x, axis=-1, keepdims=True) + 1e-08) * w

        def apply_rope(x, negate=False):
            T = x.shape[2]
            x_pass, x_rope = (x[..., :-ROPE_DIMS], x[..., -ROPE_DIMS:])
            t = jnp.arange(T, dtype=x.dtype)
            if negate:
                t = -t
            k = jnp.arange(ROPE_DIMS // 2, dtype=x.dtype)
            theta = 10000.0 ** (-2.0 * k / ROPE_DIMS)
            freqs = t[:, None] * theta[None, :]
            cos, sin = (jnp.cos(freqs), jnp.sin(freqs))
            x1, x2 = (x_rope[..., 0::2], x_rope[..., 1::2])
            rx1 = x1 * cos - x2 * sin
            rx2 = x1 * sin + x2 * cos
            rx = jnp.stack([rx1, rx2], axis=-1).reshape(x_rope.shape)
            return jnp.concatenate([x_pass, rx], axis=-1)
        B, T, d = H.shape
        nh, c = wq.shape
        Q = (H @ W_Q.T).reshape(B, T, nh, c).transpose(0, 2, 1, 3)
        K = (H @ W_K.T)[:, None]
        V = (H @ W_V.T)[:, None]
        Q = rmsnorm(Q, wq[None, :, None, :])
        K = rmsnorm(K, wk)
        V = rmsnorm(V, wv)
        Q = apply_rope(Q)
        K = apply_rope(K)[:, 0]
        V = apply_rope(V)[:, 0]
        S = jnp.einsum('bhtc,bsc->bhts', Q, K) / math.sqrt(c)
        i = jnp.arange(T)[:, None]
        j = jnp.arange(T)[None, :]
        allowed = (j <= i) & (j >= i - (N_WIN - 1))
        S = jnp.where(allowed, S, -jnp.inf)
        P = jax.nn.softmax(S, axis=-1)
        O = jnp.einsum('bhts,bsc->bhtc', P, V)
        O = apply_rope(O, negate=True)
        O_g0 = O[:, :2].transpose(0, 2, 1, 3).reshape(B, T, 2 * c)
        O_g1 = O[:, 2:].transpose(0, 2, 1, 3).reshape(B, T, 2 * c)
        p0 = O_g0 @ Wg0.T + bg0
        p1 = O_g1 @ Wg1.T + bg1
        p_all = jnp.concatenate([p0, p1], axis=-1)
        return p_all @ Wout.T + bout

    def _L2_ffn_ref(input_embeddings, router_w, w1, b1, w2, b2):
        import jax, jax.numpy as jnp
        import numpy as np
        NUM_EXPERTS = 8
        TOP_K = 2
        B, S, D = (8, 2048, 64)

        def _moe(tokens, router_w, w1, b1, w2, b2):
            N = tokens.shape[0]
            E = router_w.shape[0]
            logits = tokens.astype(jnp.float32) @ router_w.astype(jnp.float32).T
            probs = jax.nn.softmax(logits, axis=-1)
            rw, re = jax.lax.top_k(probs, TOP_K)
            if TOP_K > 1:
                rw = rw / jnp.maximum(rw.sum(-1, keepdims=True), 1e-12)
            rw = rw.astype(tokens.dtype)
            combine = jnp.zeros((N, E), tokens.dtype).at[jnp.arange(N)[:, None], re].set(rw)
            out = tokens
            for e in range(E):
                h = jax.nn.gelu(tokens @ w1[e] + b1[e], approximate=False)
                y = h @ w2[e] + b2[e]
                out = out + combine[:, e:e + 1] * y
            return out
        b, s, d = input_embeddings.shape
        tokens = input_embeddings.reshape(b * s, d)
        return _moe(tokens, router_w, w1, b1, w2, b2).reshape(b, s, d)

    def _L3_attn_ref(x, h0, numerators, denumerator):
        import jax, jax.numpy as jnp
        import numpy as np
        D_IN, D_OUT, ORDER = (64, 64, 8)
        B, L = (32, 256)
        Lx = x.shape[-2]
        a = jnp.concatenate([jnp.ones((*denumerator.shape[:-1], 1), denumerator.dtype), denumerator], axis=-1)
        b = jnp.concatenate([jnp.zeros((*numerators.shape[:-1], 1), numerators.dtype), numerators], axis=-1)
        H_trunc = jnp.fft.rfft(b, n=Lx, axis=-1) / jnp.fft.rfft(a, n=Lx, axis=-1)
        h_trunc = jnp.fft.irfft(H_trunc, n=Lx, axis=-1)
        H = jnp.fft.rfft(h_trunc, n=2 * Lx, axis=-1)
        H_causal = H[0]
        H_tf = h0.astype(H_causal.dtype) + H_causal
        X = jnp.fft.rfft(x, n=2 * Lx, axis=-2)
        Y = jnp.einsum('bli,ijl->blj', X, H_tf)
        y = jnp.fft.irfft(Y, axis=-2)
        return y[..., :Lx, :]

    def _L3_ffn_ref(x, attention_mask, wr, br, w1, b1, w2, b2):
        import jax, jax.numpy as jnp
        import numpy as np
        B, S, D = (8, 1024, 64)
        H = 4 * D
        CAPACITY = 0.5
        b, s, d = x.shape
        weights = (jnp.einsum('bsd,do->bso', x, wr) + br)[..., 0]
        k = max(1, int(CAPACITY * s))
        kk = k - 1 if k > 1 else 1
        _, idx = jax.lax.top_k(weights, k)
        sel_idx = idx[:, :kk]
        sel = jnp.take_along_axis(x, sel_idx[:, :, None], axis=1)
        h = jax.nn.gelu(jnp.einsum('bkd,dh->bkh', sel, w1) + b1)
        y = jnp.einsum('bkh,hd->bkd', h, w2) + b2
        w_sel = jnp.take_along_axis(weights, sel_idx, axis=1)
        y = y * w_sel[..., None]
        batch_idx = jnp.arange(b)[:, None]
        processed = jnp.zeros_like(x).at[batch_idx, sel_idx].set(y)
        return processed + x
    h = _L0_tok_ref(x, L0_tok_emb, L0_tok_W, L0_tok_b)
    h = h + _L0_attn_ref(_layernorm(h, axis=-1), L0_attn_Wq, L0_attn_Wkv, L0_attn_Wproj, L0_attn_bproj)
    h = h + _L0_ffn_ref(_layernorm(h, axis=-1), L0_ffn_route_id, L0_ffn_Wi, L0_ffn_bi, L0_ffn_Wr, L0_ffn_br, L0_ffn_Ws, L0_ffn_bs, L0_ffn_Wo, L0_ffn_bo)
    h = h + _L1_attn_ref(_layernorm(h, axis=-1), L1_attn_Wq, L1_attn_bq, L1_attn_Wk, L1_attn_bk, L1_attn_Wv, L1_attn_bv, L1_attn_Wl, L1_attn_bl, L1_attn_gamma, L1_attn_beta)
    h = h + _L1_ffn_ref(_layernorm(h, axis=-1), L1_ffn_gamma, L1_ffn_beta, L1_ffn_Wr, L1_ffn_br, L1_ffn_W1, L1_ffn_b1, L1_ffn_W2, L1_ffn_b2)
    h = h + _L2_attn_ref(_layernorm(h, axis=-1), L2_attn_W_Q, L2_attn_W_K, L2_attn_W_V, L2_attn_wq, L2_attn_wk, L2_attn_wv, L2_attn_Wg0, L2_attn_bg0, L2_attn_Wg1, L2_attn_bg1, L2_attn_Wout, L2_attn_bout)
    h = h + _L2_ffn_ref(_layernorm(h, axis=-1), L2_ffn_router_w, L2_ffn_w1, L2_ffn_b1, L2_ffn_w2, L2_ffn_b2)
    h = h + _L3_attn_ref(_layernorm(h, axis=-1), L3_attn_h0, L3_attn_numerators, L3_attn_denumerator)
    h = h + _L3_ffn_ref(_layernorm(h, axis=-1), L3_ffn_attention_mask, L3_ffn_wr, L3_ffn_br, L3_ffn_w1, L3_ffn_b1, L3_ffn_w2, L3_ffn_b2)
    return h

_drawn_inputs = setup_inputs


def setup_inputs(seed=0):
    import zlib

    import numpy as np

    out = dict(_drawn_inputs(seed))
    spreads = {'L0_attn_bproj': (0.0, 0.1),
     'L0_ffn_bi': (0.0, 0.1),
     'L0_ffn_bo': (0.0, 0.1),
     'L1_attn_gamma': (1.0, 0.2),
     'L1_attn_beta': (0.0, 0.1),
     'L1_ffn_br': (0.0, 0.459),
     'L2_attn_bg0': (0.0, 0.512),
     'L2_attn_bg1': (0.0, 1.968),
     'L2_attn_bout': (0.0, 0.39),
     'L2_ffn_b1': (0.0, 0.563),
     'L2_ffn_b2': (0.0, 0.378),
     'L3_ffn_b1': (0.0, 0.8),
     'L3_ffn_b2': (0.0, 2.0)}
    factors = {'L0_attn_Wq': 150.183,
     'L1_attn_Wq': 8.0,
     'L1_attn_bq': 8.0,
     'L1_attn_Wk': 8.0,
     'L1_attn_bk': 200.0,
     'L1_attn_bv': 192.406,
     'L1_attn_bl': 180.359,
     'L1_ffn_gamma': 8.0,
     'L1_ffn_beta': 8.0,
     'L1_ffn_W1': 3.535,
     'L1_ffn_b1': 8.0,
     'L1_ffn_W2': 5.756,
     'L1_ffn_b2': 11.306,
     'L2_attn_W_Q': 8.0,
     'L2_attn_W_K': 8.0,
     'L2_attn_wq': 45.847,
     'L2_attn_wk': 37.024,
     'L2_attn_wv': 29.437,
     'L3_ffn_wr': 8.0,
     'L3_ffn_w1': 8.0,
     'L3_ffn_w2': 8.0}
    for name, (base, spread) in spreads.items():
        noise = np.random.default_rng([zlib.crc32(name.encode()), seed]).standard_normal(out[name].shape)
        drawn = base * np.exp(spread * noise) if base else spread * noise
        out[name] = jnp.asarray(drawn.astype(out[name].dtype))
    for name, factor in factors.items():
        out[name] = (out[name] * factor).astype(out[name].dtype)
    return out
```

```python
from contextlib import ExitStack

import concourse.bass as bass
from concourse import mybir

F32 = mybir.dt.float32
BF16 = mybir.dt.bfloat16
I32 = mybir.dt.int32
ALU = mybir.AluOpType
ACT = mybir.ActivationFunctionType
AX = mybir.AxisListType.X

P = 128
B, T, D = 16, 256, 64
CHUNKS = B // 2
U = T // P
G4 = 2 * U
CW = G4 * D
W = 4
ITERS = CHUNKS // W
KS = 9
KC = KS * D // P
EPS = 1e-5


NORM_SEMAPHORES = "norm_halves norm_sums norm_scaled norm_var norm_rstd norm_centred normed"


def semaphores(nc, prefix, names):
    names = (NORM_SEMAPHORES + " " + names).split()
    return {name: nc.alloc_semaphore(f"{prefix}_{name}") for name in names}


def bcast(ap, axis, n):
    ap = ap.unsqueeze(axis)
    shape = list(ap.shape)
    shape[axis] = n
    return ap.broadcast_to(shape)


def chunk_of(H, it, w):
    return H[:, bass.ds(it * (W * CW) + w * CW, CW)]


def groups(ap):
    return ap.rearrange("p (g f) -> p g f", f=D)


def diagonal(ap, n, step, width):
    out = ap[:, 0:n * width].rearrange("p (n k) -> p n k", k=width).copy()
    (part, row, col) = out.ap
    return bass.AP(out.tensor, out.offset, [list(part), [step, n], list(col)])



class NormBuffers:

    def __init__(self, nc, ctx, prefix):
        def buf(name, shape):
            return ctx.enter_context(nc.sbuf_tensor(f"{prefix}_{name}", shape, F32))

        n = W * G4
        self.st = buf("halves", [P, n, 6])
        self.gap, self.mean, self.var, self.rstd = (buf(x, [P, n]) for x in ("gap", "mean", "var", "rstd"))


def norm_stats(nc, v, S, x_of, N, it):
    for w in range(W):
        for g in range(G4):
            ins = nc.vector.bn_stats(N.st[:, w * G4 + g, :], x_of(w)[:, g, :])
    ins.then_inc(S["norm_halves"], 1)
    v.wait_ge(S["norm_halves"], it + 1)
    mean_e, mean_o, m2_e, m2_o = (N.st[:, :, k] for k in (1, 4, 2, 5))
    nc.vector.tensor_tensor(N.gap[:], mean_e, mean_o, ALU.subtract).then_inc(S["norm_sums"], 1)
    nc.vector.tensor_tensor(N.mean[:], mean_e, mean_o, ALU.add).then_inc(S["norm_sums"], 1)
    nc.vector.tensor_tensor(N.var[:], m2_e, m2_o, ALU.add).then_inc(S["norm_sums"], 1)
    v.wait_ge(S["norm_sums"], it * 3 + 3)
    nc.vector.tensor_tensor(N.gap[:], N.gap[:], N.gap[:], ALU.mult).then_inc(S["norm_scaled"], 1)
    nc.vector.tensor_scalar(N.mean[:], N.mean[:], 0.5, None, ALU.mult).then_inc(S["norm_scaled"], 1)
    nc.vector.tensor_scalar(N.var[:], N.var[:], 1.0 / D, EPS, ALU.mult, ALU.add).then_inc(S["norm_scaled"], 1)
    v.wait_ge(S["norm_scaled"], it * 3 + 3)
    nc.vector.scalar_tensor_tensor(N.var[:], N.gap[:], 0.25, N.var[:], ALU.mult, ALU.add).then_inc(S["norm_var"], 1)


def norm_rstd(nc, pool, S, C, N, it):
    pool.wait_ge(S["norm_var"], it + 1)
    nc.gpsimd.tensor_tensor(N.rstd[:], N.var[:], C.minus_half[:], ALU.pow).then_inc(S["norm_rstd"], 1)


def norm_apply(nc, v, S, x_of, N, xc, xn, it):
    for w in range(W):
        nc.vector.tensor_tensor(xc[:, w], x_of(w), bcast(N.mean[:, w * G4:(w + 1) * G4], 2, D), ALU.subtract)\
            .then_inc(S["norm_centred"], 1)
    for w in range(W):
        v.wait_ge(S["norm_centred"], it * W + w + 1)
        v.wait_ge(S["norm_rstd"], it + 1)
        nc.vector.tensor_tensor(xn[:, w], xc[:, w], bcast(N.rstd[:, w * G4:(w + 1) * G4], 2, D), ALU.mult)\
            .then_inc(S["normed"], 1)



def token_convolution(nc, H, PS, C, dram):
    with ExitStack() as ctx:
        S = semaphores(nc, "tok",
                        "ids tails_zero windows_read winT_low winT_high winT_ps0 winT_ps1 winT2_low winT2_high "
                        "tailT yT_ps yT y_ps h_new")
        sb = lambda name, shape, dt=F32: ctx.enter_context(nc.sbuf_tensor(name, shape, dt))
        ids = sb("tok_ids", [P, CHUNKS * G4], I32)
        win = sb("tok_windows", [P, W, G4, KS * D])
        winT = sb("tok_windowsT", [P, W, KC, G4 * P])
        tailT = sb("tok_tailsT", [P, W, G4 * P])
        yT = sb("tok_yT", [D, W, G4 * P])
        block = ctx.enter_context(nc.Block())
        gathered = [nc.alloc_semaphore(f"tok_gathered{w}") for w in range(W)]
        w_main = C["tok_w"].rearrange("p (k f) -> p k f", f=D)

        @block.sync
        def _(sp):
            sp.dma_start(ids[:], dram["ids"]).then_inc(S["ids"], 16)

        @block.gpsimd
        def _(pool):
            nc.gpsimd.memset(tailT[:], 0.0).then_inc(S["tails_zero"], 1)
            pool.wait_ge(S["ids"], 16)
            for it in range(ITERS):
                for w in range(W):
                    if it:
                        pool.wait_ge(S["windows_read"], (it - 1) * W + w + 1)
                    for g in range(G4):
                        at = (it * W + w) * G4 + g
                        nc.gpsimd.indirect_dma_start(
                            win[:, w, g, :], None, dram["emb"],
                            bass.IndirectOffsetOnAxis(ap=ids[:, at:at + 1], axis=0)).then_inc(gathered[w], 16)

        @block.tensor
        def _(pe):
            ident = C["ident"]
            pe.wait_ge(C.sem("base"), C.count("base"))
            with pe.Fori(0, ITERS) as it:
                for r in range(KC // 2):
                    for w in range(W):
                        if r == 0:
                            pe.wait_ge(gathered[w], 16 * G4 * (it + 1))
                        else:
                            pe.wait_ge(S["winT_low"], it * W + w + 1)
                            pe.wait_ge(S["winT_high"], it * W + w + 1)
                        for k in range(2):
                            for g in range(G4):
                                at = (2 * r + k) * P
                                ins = nc.tensor.transpose(PS[w][:, k, g * P:(g + 1) * P], win[:, w, g, at:at + P],
                                                          ident)
                        ins.then_inc(S["winT_ps0"] if r == 0 else S["winT_ps1"], 1)
                for w in range(W):
                    pe.wait_ge(C.sem("base"), C.count("base"))
                    pe.wait_ge(S["winT2_low"], it * W + w + 1)
                    pe.wait_ge(S["winT2_high"], it * W + w + 1)
                    for g in range(G4):
                        ins = nc.tensor.transpose(PS[w][0:D, 0, g * P:(g + 1) * P], win[:, w, g, KC * P:], ident)
                    ins.then_inc(S["windows_read"], 1)
                for w in range(W):
                    for k in range(KC):
                        nc.tensor.matmul(PS[w][0:D, 1, :], w_main[:, k, :], winT[:, w, k, :],
                                         start=(k == 0), stop=False)
                    pe.wait_ge(S["tailT"], it * W + w + 1)
                    nc.tensor.matmul(PS[w][0:D, 1, :], w_main[:, KC, :], tailT[:, w], start=False, stop=True)\
                        .then_inc(S["yT_ps"], 1)
                for w in range(W):
                    pe.wait_ge(C.sem("base"), C.count("base"))
                    pe.wait_ge(S["yT"], it * W + w + 1)
                    for g in range(G4):
                        ins = nc.tensor.transpose(PS[w][:, 0, g * D:(g + 1) * D], yT[:, w, g * P:(g + 1) * P],
                                                  ident[0:D, 0:D])
                    ins.then_inc(S["y_ps"], 1)
                pe.wait_ge(S["h_new"], it * W + W)

        @block.scalar
        def _(act):
            act.wait_ge(S["tails_zero"], 1)
            with act.Fori(0, ITERS) as it:
                for w in range(W):
                    act.wait_ge(S["winT_ps0"], it * W + w + 1)
                    nc.scalar.copy(winT[:, w, 1, :], PS[w][:, 1, :]).then_inc(S["winT_high"], 1)
                for w in range(W):
                    act.wait_ge(S["winT_ps1"], it * W + w + 1)
                    nc.scalar.copy(winT[:, w, 3, :], PS[w][:, 1, :]).then_inc(S["winT2_high"], 1)
                for w in range(W):
                    act.wait_ge(S["windows_read"], it * W + w + 1)
                    nc.scalar.copy(tailT[0:D, w], PS[w][0:D, 0, :])\
                        .then_inc(S["tailT"], 1)
                for w in range(W):
                    act.wait_ge(S["yT_ps"], it * W + w + 1)
                    nc.scalar.copy(yT[:, w, :], PS[w][0:D, 1, :]).then_inc(S["yT"], 1)
                act.wait_ge(S["y_ps"], it * W + W)

        @block.vector
        def _(v):
            v.wait_ge(C.sem("base"), C.count("base"))
            with v.Fori(0, ITERS) as it:
                for w in range(W):
                    v.wait_ge(S["winT_ps0"], it * W + w + 1)
                    nc.vector.tensor_copy(winT[:, w, 0, :], PS[w][:, 0, :]).then_inc(S["winT_low"], 1)
                for w in range(W):
                    v.wait_ge(S["winT_ps1"], it * W + w + 1)
                    nc.vector.tensor_copy(winT[:, w, 2, :], PS[w][:, 0, :]).then_inc(S["winT2_low"], 1)
                for w in range(W):
                    v.wait_ge(S["y_ps"], it * W + w + 1)
                    nc.vector.tensor_tensor(groups(chunk_of(H, it, w)), groups(PS[w][:, 0, 0:CW]),
                                            bcast(C["tok_b"], 1, G4), ALU.add).then_inc(S["h_new"], 1)



def linear_attention(nc, H, PS, C, dram):
    with ExitStack() as ctx:
        S = semaphores(nc, "lin",
                        "ones qk_ps neg expneg qk ctx_ps cm attn_ps den inv aT proj_ps proj h_new xT_ps xT v_ps "
                        "v1")
        sb = lambda name, shape, dt=F32: ctx.enter_context(nc.sbuf_tensor("lin_" + name, shape, dt))
        N = NormBuffers(nc, ctx, "lin")
        xc, xn = sb("xc", [P, W, G4, D]), sb("xn", [P, W, G4, D])
        xT = sb("xT", [P, W, U, P])
        neg = sb("neg", [P, W, 2, U * P])
        qk = sb("qk", [P, W, 2, U * P])
        v1 = sb("v1", [P, W, U, 2, P])
        cm = sb("cm", [P, W, 2, P])
        num = sb("num", [P, W, U * P])
        inv = sb("inv", [P, W, U * P])
        aT = sb("aT", [P, W, U, P])
        block = ctx.enter_context(nc.Block())
        hx = lambda it: (lambda w: groups(chunk_of(H, it, w)))

        @block.gpsimd
        def _(pool):
            nc.gpsimd.memset(v1[:, :, :, 1, :], 1.0).then_inc(S["ones"], 1)
            with pool.Fori(0, ITERS) as it:
                norm_rstd(nc, pool, S, C, N, it)

        @block.vector
        def _(v):
            v.wait_ge(S["ones"], 1)
            v.wait_ge(C.sem("early"), C.count("early"))
            with v.Fori(0, ITERS) as it:
                norm_stats(nc, v, S, hx(it), N, it)
                norm_apply(nc, v, S, hx(it), N, xc, xn, it)
                for w in range(W):
                    v.wait_ge(S["qk_ps"], it * W + w + 1)
                    nc.vector.tensor_scalar(neg[:, w], PS[w][:, 0, :].rearrange("p (a n) -> p a n", a=2),
                                            0.0, None, ALU.min).then_inc(S["neg"], 1)
                for w in range(W):
                    v.wait_ge(S["expneg"], it * W + w + 1)
                    nc.vector.scalar_tensor_tensor(qk[:, w].rearrange("p a n -> p (a n)"), PS[w][:, 0, :], 0.0,
                                                   neg[:, w].rearrange("p a n -> p (a n)"), ALU.max, ALU.add)\
                        .then_inc(S["qk"], 1)
                for w in range(W):
                    v.wait_ge(S["ctx_ps"], it * W + w + 1)
                    nc.vector.tensor_tensor(cm[:, w], PS[w][:, 1, 0:2 * P].rearrange("p (a n) -> p a n", a=2),
                                            bcast(C["lin_mask"], 1, 2), ALU.mult).then_inc(S["cm"], 1)
                for w in range(W):
                    v.wait_ge(S["attn_ps"], it * W + w + 1)
                    nc.vector.tensor_scalar(num[:, w], PS[w][:, 0, U * P:2 * U * P], 1e-6, None, ALU.max)\
                        .then_inc(S["den"], 1)
                for w in range(W):
                    v.wait_ge(S["den"], it * W + w + 1)
                    nc.vector.reciprocal(inv[:, w], num[:, w]).then_inc(S["inv"], 1)
                for w in range(W):
                    v.wait_ge(S["inv"], it * W + w + 1)
                    nc.vector.tensor_tensor(aT[:, w].rearrange("p u q -> p (u q)"), PS[w][:, 0, 0:U * P], inv[:, w],
                                            ALU.mult).then_inc(S["aT"], 1)
                for w in range(W):
                    v.wait_ge(S["proj_ps"], it * W + w + 1)
                    nc.vector.tensor_tensor(xc[:, w], groups(PS[w][:, 1, 0:CW]), bcast(C["lin_b"], 1, G4), ALU.add)\
                        .then_inc(S["proj"], 1)
                for w in range(W):
                    v.wait_ge(S["proj"], it * W + w + 1)
                    x = hx(it)(w)
                    nc.vector.tensor_tensor(x, x, xc[:, w], ALU.add).then_inc(S["h_new"], 1)
                v.wait_ge(S["h_new"], it * W + W)

        @block.scalar
        def _(act):
            with act.Fori(0, ITERS) as it:
                for w in range(W):
                    act.wait_ge(S["xT_ps"], it * W + w + 1)
                    nc.scalar.copy(xT[:, w].rearrange("p u q -> p (u q)"), PS[w][:, 0, 0:U * P]).then_inc(S["xT"], 1)
                for w in range(W):
                    act.wait_ge(S["neg"], it * W + w + 1)
                    nc.scalar.activation(neg[:, w], neg[:, w], ACT.Exp).then_inc(S["expneg"], 1)
                    act.wait_ge(S["v_ps"], it * W + w + 1)
                    nc.scalar.copy(v1[:, w, :, 0, :], PS[w][:, 1, 0:U * P].rearrange("p (u n) -> p u n", u=U))\
                        .then_inc(S["v1"], 1)

        @block.tensor
        def _(pe):
            ident = C["ident"]
            pe.wait_ge(C.sem("base"), C.count("base"))
            pe.wait_ge(C.sem("early"), C.count("early"))
            with pe.Fori(0, ITERS) as it:
                for w in range(W):
                    pe.wait_ge(S["normed"], it * W + w + 1)
                    for u in range(U):
                        ins = nc.tensor.transpose(PS[w][:, 0, u * P:(u + 1) * P],
                                                  xn[:, w, 2 * u:2 * u + 2, :].rearrange("p g f -> p (g f)"), ident)
                    ins.then_inc(S["xT_ps"], 1)
                for w in range(W):
                    pe.wait_ge(S["xT"], it * W + w + 1)
                    nc.tensor.matmul(PS[w][:, 0, 0:U * P], C["lin_q"], xT[:, w].rearrange("p u q -> p (u q)"),
                                     start=True, stop=True)
                    for u in range(U):
                        ins = nc.tensor.matmul(PS[w][:, 0, (U + u) * P:(U + u + 1) * P], xT[:, w, u, :], C["lin_k"],
                                               start=True, stop=True)
                    ins.then_inc(S["qk_ps"], 1)
                    for u in range(U):
                        ins = nc.tensor.matmul(PS[w][:, 1, u * P:(u + 1) * P], xT[:, w, u, :], C["lin_v"],
                                               start=True, stop=True)
                    ins.then_inc(S["v_ps"], 1)
                for w in range(W):
                    pe.wait_ge(S["v1"], it * W + w + 1)
                    pe.wait_ge(S["qk"], it * W + w + 1)
                    for u in range(U):
                        ins = nc.tensor.matmul(PS[w][:, 1, 0:2 * P], qk[:, w, 1, u * P:(u + 1) * P],
                                               v1[:, w, u].rearrange("p a n -> p (a n)"), start=(u == 0),
                                               stop=(u == U - 1))
                    ins.then_inc(S["ctx_ps"], 1)
                for w in range(W):
                    pe.wait_ge(S["cm"], it * W + w + 1)
                    for a in range(2):
                        ins = nc.tensor.matmul(PS[w][:, 0, a * U * P:(a + 1) * U * P], cm[:, w, a, :], qk[:, w, 0, :],
                                               start=True, stop=True)
                    ins.then_inc(S["attn_ps"], 1)
                for w in range(W):
                    pe.wait_ge(S["aT"], it * W + w + 1)
                    for u in range(U):
                        ins = nc.tensor.matmul(PS[w][:, 1, u * P:(u + 1) * P], aT[:, w, u, :], C["lin_o"],
                                               start=True, stop=True)
                    ins.then_inc(S["proj_ps"], 1)



HID = 128
EXPERTS = 16
SEG = 64
SEGS = 2 * T // SEG
RW = 2 * HID + 2


def load_experts(sp, dram, route, routed, S, it):
    for w in range(W):
        for j in range(SEGS):
            e = sp.value_load(route[0:1, bass.ds(it * (W * SEGS) + (w * SEGS + j), 1)], min_val=0, max_val=EXPERTS - 1)
            sp.dma_start(routed[:, w, j, :], dram["routed"][bass.ds(e * P, P), :]).then_inc(S[w], 16)


def routed_ffn(nc, H, PS, C, dram):
    with ExitStack() as ctx:
        S = semaphores(nc, "rff",
                        "route h_new bias z0_ps z1_ps z0 z1 o_ps xT_ps xT hid_ps h0 h1 h2 oT_ps oT")
        sb = lambda name, shape, dt=F32: ctx.enter_context(nc.sbuf_tensor("rff_" + name, shape, dt))
        N = NormBuffers(nc, ctx, "rff")
        xc, xn = sb("xc", [P, W, G4, D]), sb("xn", [P, W, G4, D])
        route = sb("route", [1, CHUNKS * SEGS], I32)
        routed = sb("routed", [P, W, SEGS, RW])
        bias = sb("bias", [P, W, 2, SEGS])
        xT = sb("xT", [P, W, U * P])
        hT = [sb(f"hT{l}", [P, W, 2 * T]) for l in range(3)]
        oT = sb("oT", [D, W, 2 * T])
        experts = [nc.alloc_semaphore(f"rff_experts{w}") for w in range(W)]
        block = ctx.enter_context(nc.Block())
        hx = lambda it: (lambda w: groups(chunk_of(H, it, w)))

        @block.sync
        def _(sp):
            sp.dma_start(route[:], dram["route"]).then_inc(S["route"], 16)
            sp.wait_ge(S["route"], 16)
            load_experts(sp, dram, route, routed, experts, 0)
            with sp.Fori(1, ITERS) as it:
                sp.wait_ge(S["h_new"], it * W)
                load_experts(sp, dram, route, routed, experts, it)

        @block.gpsimd
        def _(pool):
            pool.wait_ge(C.sem("early"), C.count("early"))
            with pool.Fori(0, ITERS) as it:
                norm_rstd(nc, pool, S, C, N, it)
                for w in range(W):
                    pool.wait_ge(experts[w], 16 * SEGS * (it + 1))
                    nc.gpsimd.tensor_tensor(bias[:, w], routed[:, w, :, 2 * HID:].rearrange("p j l -> p l j"),
                                            bcast(C["rff_bs"], 2, SEGS), ALU.add).then_inc(S["bias"], 1)

        @block.vector
        def _(v):
            with v.Fori(0, ITERS) as it:
                norm_stats(nc, v, S, hx(it), N, it)
                norm_apply(nc, v, S, hx(it), N, xc, xn, it)
                for l in range(2):
                    for w in range(W):
                        v.wait_ge(S["bias"], it * W + w + 1)
                        v.wait_ge(S["z0_ps"] if l == 0 else S["z1_ps"], it * W + w + 1)
                        z = hT[l + 1][:, w].rearrange("p (j n) -> p j n", n=SEG)
                        nc.vector.tensor_tensor(z, PS[w][:, l, :].rearrange("p (j n) -> p j n", n=SEG),
                                                bcast(bias[:, w, l, :], 2, SEG), ALU.add)\
                            .then_inc(S["z0"] if l == 0 else S["z1"], 1)
                for w in range(W):
                    v.wait_ge(S["o_ps"], it * W + w + 1)
                    x = hx(it)(w)
                    nc.vector.tensor_tensor(x, x, groups(PS[w][:, 1, 0:CW]), ALU.add).then_inc(S["h_new"], 1)
                v.wait_ge(S["h_new"], it * W + W)

        @block.scalar
        def _(act):
            act.wait_ge(C.sem("early"), C.count("early"))
            with act.Fori(0, ITERS) as it:
                for w in range(W):
                    act.wait_ge(S["xT_ps"], it * W + w + 1)
                    nc.scalar.copy(xT[:, w], PS[w][:, 0, 0:U * P]).then_inc(S["xT"], 1)
                for w in range(W):
                    act.wait_ge(S["hid_ps"], it * W + w + 1)
                    nc.scalar.activation(hT[0][:, w], PS[w][:, 1, :], ACT.Relu, bias=C["rff_bi"]).then_inc(S["h0"], 1)
                for w in range(W):
                    act.wait_ge(S["z0"], it * W + w + 1)
                    nc.scalar.activation(hT[1][:, w], hT[1][:, w], ACT.Relu).then_inc(S["h1"], 1)
                for w in range(W):
                    act.wait_ge(S["z1"], it * W + w + 1)
                    nc.scalar.activation(hT[2][:, w], hT[2][:, w], ACT.Relu).then_inc(S["h2"], 1)
                for w in range(W):
                    act.wait_ge(S["oT_ps"], it * W + w + 1)
                    nc.scalar.activation(oT[:, w], PS[w][0:D, 0, :], ACT.Identity, bias=C["rff_bo"][0:D, :])\
                        .then_inc(S["oT"], 1)

        @block.tensor
        def _(pe):
            ident = C["ident"]
            shared = C["rff_shared"].rearrange("p (l n) -> p l n", l=2)
            first = C["rff_wi"].rearrange("p (h n) -> p h n", h=2)
            pe.wait_ge(C.sem("early"), C.count("early"))
            with pe.Fori(0, ITERS) as it:
                for w in range(W):
                    pe.wait_ge(S["normed"], it * W + w + 1)
                    for u in range(U):
                        ins = nc.tensor.transpose(PS[w][:, 0, u * P:(u + 1) * P],
                                                  xn[:, w, 2 * u:2 * u + 2, :].rearrange("p g f -> p (g f)"), ident)
                    ins.then_inc(S["xT_ps"], 1)
                for w in range(W):
                    pe.wait_ge(S["xT"], it * W + w + 1)
                    for half in range(2):
                        ins = nc.tensor.matmul(PS[w][:, 1, half * T:(half + 1) * T], first[:, half, :], xT[:, w],
                                               start=True, stop=True)
                    ins.then_inc(S["hid_ps"], 1)
                for l in range(2):
                    for w in range(W):
                        pe.wait_ge(S["h0"] if l == 0 else S["h1"], it * W + w + 1)
                        pe.wait_ge(experts[w], 16 * SEGS * (it + 1))
                        nc.tensor.matmul(PS[w][:, l, :], shared[:, l, :], hT[l][:, w], start=True, stop=False)
                        nc.tensor.matmul(PS[w][:, l, :], ident, hT[l][:, w], start=False, stop=False)
                        for j in range(SEGS):
                            at = slice(j * SEG, (j + 1) * SEG)
                            ins = nc.tensor.matmul(PS[w][:, l, at], routed[:, w, j, l * HID:(l + 1) * HID],
                                                   hT[l][:, w, at], start=False, stop=(j == SEGS - 1))
                        ins.then_inc(S["z0_ps"] if l == 0 else S["z1_ps"], 1)
                for w in range(W):
                    pe.wait_ge(S["h2"], it * W + w + 1)
                    nc.tensor.matmul(PS[w][0:D, 0, :], C["rff_wo"], hT[2][:, w], start=True, stop=True)\
                        .then_inc(S["oT_ps"], 1)
                for w in range(W):
                    pe.wait_ge(C.sem("base"), C.count("base"))
                    pe.wait_ge(S["oT"], it * W + w + 1)
                    for g in range(G4):
                        at = (g % 2) * T + (g // 2) * P
                        ins = nc.tensor.transpose(PS[w][:, 1, g * D:(g + 1) * D], oT[:, w, at:at + P],
                                                  ident[0:D, 0:D])
                    ins.then_inc(S["o_ps"], 1)



def batchnorm_attention(nc, H, PS, C, dram):
    with ExitStack() as ctx:
        S = semaphores(nc, "bna",
                        "zeros h_plus_x bn_var bn_rstd v_ps v score_ps top bound probT_ps probT_low inv out_ps "
                        "scaled attn FT sum1 sum1_ps sum1_moved sum2 sum2_ps bn_mean bn_centred bn_squared "
                        "var_ps bn_gain y_ps h_new xT_ps xT qk_ps qk prob probT_high aT_ps aT attnT_ps y")
        sb = lambda name, shape, dt=F32: ctx.enter_context(nc.sbuf_tensor("bna_" + name, shape, dt))
        N = NormBuffers(nc, ctx, "bna")
        xc, xn = sb("xc", [P, W, G4, D]), sb("xn", [P, W, G4, D])
        xT = sb("xT", [P, W, U * P])
        q = sb("q", [P, W, 2, T])
        kT = sb("kT", [P, W, T])
        v = sb("v", [P, W, U, 2, P])
        top, total = sb("top", [P, W, 4]), sb("total", [P, W, 4])
        inv = sb("inv", [P, W, 4])
        prob = sb("prob", [P, W, 4, T])
        probT = sb("probT", [P, W, 2, 2 * T])
        aT = sb("aT", [P, W, T])
        scaled = sb("scaled", [P, W, G4, D])
        attn = sb("attn", [P, W, G4, D])
        FT = sb("FT", [P, CHUNKS * T])
        junk = sb("junk", [P, CHUNKS * T])
        total1, total2 = sb("total1", [P, 1]), sb("total2", [P, 1])
        mean, var, gain = sb("bn_mean", [P, 1]), sb("bn_var", [P, 1]), sb("bn_gain", [P, 1])
        block = ctx.enter_context(nc.Block())
        hx = lambda it: (lambda w: groups(chunk_of(H, it, w)))
        TOKENS = B * T
        lower, upper = slice(0, D), slice(D, P)

        @block.gpsimd
        def _(pool):
            nc.gpsimd.memset(q[:], 0.0).then_inc(S["zeros"], 1)
            nc.gpsimd.memset(v[:], 0.0).then_inc(S["zeros"], 1)
            with pool.Fori(0, ITERS) as it:
                norm_rstd(nc, pool, S, C, N, it)
                for w in range(W):
                    pool.wait_ge(S["normed"], it * W + w + 1)
                    x = hx(it)(w)
                    nc.gpsimd.tensor_tensor(x, x, xn[:, w], ALU.add).then_inc(S["h_plus_x"], 1)
            pool.wait_ge(S["bn_var"], 1)
            nc.gpsimd.tensor_tensor(gain[:], var[:], C.minus_half[:, 0:1], ALU.pow).then_inc(S["bn_rstd"], 1)

        @block.vector
        def _(vec):
            vec.wait_ge(S["zeros"], 2)
            vec.wait_ge(C.sem("early"), C.count("early"))
            with vec.Fori(0, ITERS) as it:
                norm_stats(nc, vec, S, hx(it), N, it)
                norm_apply(nc, vec, S, hx(it), N, xc, xn, it)
                for w in range(W):
                    vec.wait_ge(S["v_ps"], it * W + w + 1)
                    ps = PS[w][:, 1, 0:CW].rearrange("p (u h f) -> p u h f", u=U, h=2)
                    for half in range(2):
                        ins = nc.vector.tensor_tensor(v[:, w, :, half, half * D:(half + 1) * D], ps[:, :, half, :],
                                                      bcast(C["bna_bv"], 1, U), ALU.add)
                    ins.then_inc(S["v"], 1)
                for w in range(W):
                    vec.wait_ge(S["score_ps"], it * W + w + 1)
                    nc.vector.tensor_reduce(top[:, w], PS[w][:].rearrange("p h (u k) -> p (h u) k", u=U), AX, ALU.max)\
                        .then_inc(S["top"], 1)
                for w in range(W):
                    vec.wait_ge(S["top"], it * W + w + 1)
                    nc.vector.tensor_scalar(top[:, w], top[:, w], -1.0 / D, None, ALU.mult).then_inc(S["bound"], 1)
                for w in range(W):
                    vec.wait_ge(S["probT_ps"], it * W + w + 1)
                    nc.vector.tensor_copy(probT[:, w, 0, :], PS[w][:, 0, :]).then_inc(S["probT_low"], 1)
                    nc.vector.reciprocal(inv[:, w], total[:, w]).then_inc(S["inv"], 1)
                for w in range(W):
                    vec.wait_ge(S["inv"], it * W + w + 1)
                    vec.wait_ge(S["out_ps"], it * W + w + 1)
                    nc.vector.tensor_tensor(scaled[:, w].rearrange("p (u h) f -> p u h f", u=U),
                                            PS[w][:, 1, 0:CW].rearrange("p (u h f) -> p u h f", u=U, h=2),
                                            bcast(inv[:, w].rearrange("p (h u) -> p u h", h=2), 3, D), ALU.mult)\
                        .then_inc(S["scaled"], 1)
                for w in range(W):
                    vec.wait_ge(S["scaled"], it * W + w + 1)
                    nc.vector.tensor_tensor(attn[:, w], scaled[:, w], bcast(C["bna_bl"], 1, G4), ALU.add)\
                        .then_inc(S["attn"], 1)
                vec.wait_ge(S["FT"], it * W + W)
                vec.wait_ge(S["h_plus_x"], it * W + W)
            vec.wait_ge(S["FT"], CHUNKS)
            nc.vector.tensor_scalar(junk[lower, :], FT[lower, :], 0.0, 0.0, ALU.add, ALU.add,
                                    accum_out=total1[lower, :]).then_inc(S["sum1"], 1)
            vec.wait_ge(S["sum1_ps"], 1)
            nc.vector.tensor_copy(total2[:], PS[0][:, 0, 0:1]).then_inc(S["sum1_moved"], 1)
            vec.wait_ge(S["sum1_moved"], 1)
            nc.vector.tensor_scalar(junk[upper, :], FT[upper, :], 0.0, total2[upper, :], ALU.add, ALU.add,
                                    accum_out=total1[upper, :]).then_inc(S["sum2"], 1)
            vec.wait_ge(S["sum2_ps"], 1)
            nc.vector.tensor_scalar(mean[:], PS[0][:, 0, 1:2], 1.0 / TOKENS, None, ALU.mult).then_inc(S["bn_mean"], 1)
            vec.wait_ge(S["bn_mean"], 1)
            nc.vector.tensor_scalar(FT[:], FT[:], mean[:], None, ALU.subtract).then_inc(S["bn_centred"], 1)
            vec.wait_ge(S["bn_centred"], 1)
            nc.vector.tensor_tensor_reduce(junk[:], FT[:], FT[:], 1.0, 0.0, ALU.mult, ALU.add, total2[:])\
                .then_inc(S["bn_squared"], 1)
            vec.wait_ge(S["var_ps"], 1)
            nc.vector.tensor_scalar(var[:], PS[0][:, 0, 2:3], 1.0 / TOKENS, EPS, ALU.mult, ALU.add).then_inc(S["bn_var"], 1)
            vec.wait_ge(S["bn_rstd"], 1)
            nc.vector.tensor_tensor(gain[:], gain[:], C["bna_gamma"], ALU.mult).then_inc(S["bn_gain"], 1)
            vec.wait_ge(S["h_plus_x"], CHUNKS)
            for c in range(CHUNKS):
                at = slice(c * CW, (c + 1) * CW)
                vec.wait_ge(S["y_ps"], c + 1)
                nc.vector.tensor_tensor(H[:, at], H[:, at], PS[c % W][:, 1, 0:CW], ALU.add).then_inc(S["h_new"], 1)

        @block.scalar
        def _(act):
            act.wait_ge(S["zeros"], 2)
            act.wait_ge(C.sem("early"), C.count("early"))
            with act.Fori(0, ITERS) as it:
                for w in range(W):
                    act.wait_ge(S["xT_ps"], it * W + w + 1)
                    nc.scalar.copy(xT[:, w], PS[w][:, 0, 0:U * P]).then_inc(S["xT"], 1)
                for w in range(W):
                    act.wait_ge(S["qk_ps"], it * W + w + 1)
                    for half in range(2):
                        rows = slice(half * D, (half + 1) * D)
                        nc.scalar.activation(q[rows, w, half, :], PS[w][rows, 0, 0:T], ACT.Identity,
                                             bias=C["bna_bq"][rows, :])
                    nc.scalar.activation(kT[:, w], PS[w][:, 0, T:2 * T], ACT.Identity, bias=C["bna_bk"])\
                        .then_inc(S["qk"], 1)
                for w in range(W):
                    act.wait_ge(S["bound"], it * W + w + 1)
                    for s in range(4):
                        ins = nc.scalar.activation(prob[:, w, s, :], PS[w][:, s // 2, (s % 2) * T:(s % 2 + 1) * T],
                                                   ACT.Exp, bias=top[:, w, s:s + 1], scale=1.0 / D,
                                                   accum_out=total[:, w, s:s + 1])
                    ins.then_inc(S["prob"], 1)
                for w in range(W):
                    act.wait_ge(S["probT_ps"], it * W + w + 1)
                    nc.scalar.copy(probT[:, w, 1, :], PS[w][:, 1, :]).then_inc(S["probT_high"], 1)
                for w in range(W):
                    act.wait_ge(S["aT_ps"], it * W + w + 1)
                    nc.scalar.copy(aT[:, w], PS[w][:, 0, 0:T]).then_inc(S["aT"], 1)
                for w in range(W):
                    act.wait_ge(S["attnT_ps"], it * W + w + 1)
                    nc.scalar.copy(FT[:, bass.ds(it * (W * T) + w * T, T)], PS[w][:, 0, 0:T]).then_inc(S["FT"], 1)
            act.wait_ge(S["bn_gain"], 1)
            for c in range(CHUNKS):
                at = slice(c * T, (c + 1) * T)
                nc.scalar.activation(junk[:, at], FT[:, at], ACT.Relu, bias=C["bna_beta"], scale=gain[:]).then_inc(S["y"], 1)

        @block.tensor
        def _(pe):
            ident = C["ident"]
            pe.wait_ge(C.sem("base"), C.count("base"))
            pe.wait_ge(C.sem("early"), C.count("early"))
            with pe.Fori(0, ITERS) as it:
                for w in range(W):
                    pe.wait_ge(S["normed"], it * W + w + 1)
                    for u in range(U):
                        ins = nc.tensor.transpose(PS[w][:, 0, u * P:(u + 1) * P],
                                                  xn[:, w, 2 * u:2 * u + 2, :].rearrange("p g f -> p (g f)"), ident)
                    ins.then_inc(S["xT_ps"], 1)
                for w in range(W):
                    pe.wait_ge(S["xT"], it * W + w + 1)
                    nc.tensor.matmul(PS[w][:, 0, 0:T], C["bna_wq"], xT[:, w], start=True, stop=True)
                    nc.tensor.matmul(PS[w][:, 0, T:2 * T], C["bna_wk"], xT[:, w], start=True, stop=True)\
                        .then_inc(S["qk_ps"], 1)
                    for u in range(U):
                        ins = nc.tensor.matmul(PS[w][:, 1, u * P:(u + 1) * P], xT[:, w, u * P:(u + 1) * P], C["bna_wv"],
                                               start=True, stop=True)
                    ins.then_inc(S["v_ps"], 1)
                for w in range(W):
                    pe.wait_ge(S["qk"], it * W + w + 1)
                    pe.wait_ge(S["v"], it * W + w + 1)
                    for half in range(2):
                        for u in range(U):
                            ins = nc.tensor.matmul(PS[w][:, half, u * T:(u + 1) * T], q[:, w, half, u * P:(u + 1) * P],
                                                   kT[:, w], start=True, stop=True)
                    ins.then_inc(S["score_ps"], 1)
                for w in range(W):
                    pe.wait_ge(S["prob"], it * W + w + 1)
                    for half in range(2):
                        for kt in range(U):
                            for u in range(U):
                                at = (kt * U + u) * P
                                ins = nc.tensor.transpose(PS[w][:, half, at:at + P],
                                                          prob[:, w, half * U + u, kt * P:(kt + 1) * P], ident)
                    ins.then_inc(S["probT_ps"], 1)
                for w in range(W):
                    pe.wait_ge(S["probT_low"], it * W + w + 1)
                    pe.wait_ge(S["probT_high"], it * W + w + 1)
                    for half in range(2):
                        for kt in range(U):
                            ins = nc.tensor.matmul(PS[w][:, 0, 0:T], v[:, w, kt, half, :],
                                                   probT[:, w, half, kt * T:(kt + 1) * T],
                                                   start=(half + kt == 0), stop=(half * kt == 1))
                    ins.then_inc(S["aT_ps"], 1)
                for w in range(W):
                    pe.wait_ge(S["aT"], it * W + w + 1)
                    for u in range(U):
                        ins = nc.tensor.matmul(PS[w][:, 1, u * P:(u + 1) * P], aT[:, w, u * P:(u + 1) * P], C["bna_wl"],
                                               start=True, stop=True)
                    ins.then_inc(S["out_ps"], 1)
                for w in range(W):
                    pe.wait_ge(S["attn"], it * W + w + 1)
                    for u in range(U):
                        ins = nc.tensor.transpose(PS[w][:, 0, u * P:(u + 1) * P],
                                                  attn[:, w, 2 * u:2 * u + 2, :].rearrange("p g f -> p (g f)"), ident)
                    ins.then_inc(S["attnT_ps"], 1)
            halves = C["bna_halves"].rearrange("p (k n) -> p k n", k=3)
            pe.wait_ge(S["sum1"], 1)
            nc.tensor.matmul(PS[0][:, 0, 0:1], halves[lower, 0, :], total1[lower, :], start=True, stop=True)\
                .then_inc(S["sum1_ps"], 1)
            pe.wait_ge(S["sum2"], 1)
            nc.tensor.matmul(PS[0][:, 0, 1:2], halves[:, 1, :], total1[:], start=True, stop=True)\
                .then_inc(S["sum2_ps"], 1)
            pe.wait_ge(S["bn_squared"], 1)
            nc.tensor.matmul(PS[0][:, 0, 2:3], halves[:, 2, :], total2[:], start=True, stop=True)\
                .then_inc(S["var_ps"], 1)
            for c in range(CHUNKS):
                pe.wait_ge(S["y"], c + 1)
                if c >= W:
                    pe.wait_ge(S["h_new"], c - W + 1)
                for u in range(U):
                    at = c * T + u * P
                    ins = nc.tensor.transpose(PS[c % W][:, 1, u * P:(u + 1) * P], junk[:, at:at + P], ident)
                ins.then_inc(S["y_ps"], 1)



E8 = 8
PARTS = 3
GR = PARTS * G4 * E8


def split_bf16(nc, v, src, out_f, tmp_b, rest, ready, n0):
    steps = [
        lambda: nc.vector.tensor_copy(tmp_b[0], src),
        lambda: nc.vector.tensor_copy(out_f[0], tmp_b[0]),
        lambda: nc.vector.tensor_tensor(rest, src, out_f[0], ALU.subtract),
        lambda: nc.vector.tensor_copy(tmp_b[1], rest),
        lambda: nc.vector.tensor_copy(out_f[1], tmp_b[1]),
        lambda: nc.vector.tensor_tensor(out_f[2], rest, out_f[1], ALU.subtract),
    ]
    for k, step in enumerate(steps):
        step().then_inc(ready, 1)
        v.wait_ge(ready, n0 + k + 1)


def gate_top2(nc, v, S, it, key, val, prio, t):
    n = [0]

    def done(ins):
        ins.then_inc(S["gate"], 1)
        n[0] += 1
        v.wait_ge(S["gate"], it * GATE_STEPS + n[0])

    e8 = lambda ap: bcast(ap, 2, E8)
    prio_b = bcast(prio, 1, W * G4)
    for best in (t.first, t.second):
        done(nc.vector.tensor_reduce(t.m[:], key, AX, ALU.max))
        done(nc.vector.tensor_tensor(t.eq[:], key, e8(t.m[:]), ALU.is_equal))
        done(nc.vector.tensor_tensor(t.eq[:], t.eq[:], prio_b, ALU.mult))
        done(nc.vector.tensor_reduce(t.m[:], t.eq[:], AX, ALU.max))
        done(nc.vector.tensor_tensor(best[:], t.eq[:], e8(t.m[:]), ALU.is_equal))
        if best is t.first:
            done(nc.vector.scalar_tensor_tensor(t.rest[:], best[:], -1e30, key, ALU.mult, ALU.add))
            key = t.rest[:]
    done(nc.vector.tensor_tensor(t.first[:], t.first[:], t.second[:], ALU.add))
    done(nc.vector.tensor_tensor(t.w[:], val, t.first[:], ALU.mult))
    done(nc.vector.tensor_reduce(t.m[:], t.w[:], AX, ALU.add))
    done(nc.vector.tensor_scalar(t.m[:], t.m[:], 1e-12, None, ALU.max))
    done(nc.vector.reciprocal(t.m[:], t.m[:]))
    done(nc.vector.tensor_tensor(t.w[:], t.w[:], e8(t.m[:]), ALU.mult))


GATE_STEPS = 17


class GateBuffers:
    def __init__(self, sb):
        small, wide = [P, W * G4], [P, W * G4, E8]
        self.m = sb("gate_m", small)
        self.logit, self.e, self.eq, self.first, self.second, self.rest, self.w = (
            sb("gate_" + x, wide) for x in ("logit", "e", "eq", "first", "second", "rest", "w"))


def gelu_moe(nc, H, PS, C, dram, pre, hid, again):
    per = P // hid
    SL = E8 // per
    with ExitStack() as ctx:
        S = semaphores(nc, pre,
                        "gate y_ps h_plus_x h_new gw_read yT b2_split b2 logit_ps logit top shifted exp soft "
                        "parts gT_ps gT gelu gate_ps gw sel xT_ps xT hid_ps")
        sb = lambda name, shape, dt=F32: ctx.enter_context(nc.sbuf_tensor(f"{pre}_{name}", shape, dt))
        N = NormBuffers(nc, ctx, pre)
        xc, xn = sb("xc", [P, W, G4, D]), sb("xn", [P, W, G4, D])
        if again:
            S2, N2 = semaphores(nc, pre + "2", ""), NormBuffers(nc, ctx, pre + "2")
            x2 = sb("x2", [P, W, G4, D])
        else:
            S2, x2 = S, xn
        xT = sb("xT", [P, W, T])
        t = GateBuffers(sb)
        t_b = [sb(f"gate_b{k}", [P, W * G4, E8], BF16) for k in range(2)]
        parts = sb("parts", [P, W, PARTS, G4 * E8])
        rest = sb("parts_rest", [P, W, G4 * E8])
        gT = sb("gT", [GR, W, 2 * T], BF16)
        sel = sb("sel", [GR, SL * P], BF16)
        b2f, b2b, b2r = sb("b2f", [GR, PARTS, D]), sb("b2b", [GR, PARTS, D], BF16), sb("b2r", [GR, D])
        b2t = [sb(f"b2t{k}", [GR, D], BF16) for k in range(2)]
        g = sb("g", [P, 2, 2 * T])
        gw = sb("gw", [P, 2, 2 * T])
        yT = sb("yT", [D, W, 2 * T])
        block = ctx.enter_context(nc.Block())
        hx = lambda it: (lambda w: groups(chunk_of(H, it, w)))
        banks = [PS[k // 2][:, k % 2, :] for k in range(2 * W)]
        hid_bank, gate_bank, y_bank = banks[0:3], banks[3:6], banks[6:8]
        steps = [(w, s) for w in range(W) for s in range(SL)]
        n_steps = len(steps)

        def add_output(v, it, w):
            v.wait_ge(S["y_ps"], it * W + w + 1)
            if not again:
                v.wait_ge(S["h_plus_x"], it * W + w + 1)
            x = hx(it)(w)
            nc.vector.tensor_tensor(x, x, groups(y_bank[w % 2][:, 0:CW]), ALU.add).then_inc(S["h_new"], 1)

        def copy_output(act, it, w):
            act.wait_ge(S["gw_read"], it * n_steps + (w + 1) * SL)
            nc.scalar.copy(yT[:, w], y_bank[w % 2][0:D, :]).then_inc(S["yT"], 1)

        @block.sync
        def _(sp):
            C.load(sp, "win" if again else "rat")

        @block.gpsimd
        def _(pool):
            with pool.Fori(0, ITERS) as it:
                norm_rstd(nc, pool, S, C, N, it)
                if again:
                    norm_rstd(nc, pool, S2, C, N2, it)
                else:
                    for w in range(W):
                        pool.wait_ge(S["normed"], it * W + w + 1)
                        x = hx(it)(w)
                        nc.gpsimd.tensor_tensor(x, x, xn[:, w], ALU.add).then_inc(S["h_plus_x"], 1)

        @block.vector
        def _(v):
            v.wait_ge(C.sem(pre), C.count(pre))
            split_bf16(nc, v, C[pre + "_b2"][0:GR, :], [b2f[:, k, :] for k in range(PARTS)], [b[:] for b in b2t],
                       b2r[:], S["b2_split"], 0)
            nc.vector.tensor_copy(b2b[:], b2f[:]).then_inc(S["b2"], 1)
            with v.Fori(0, ITERS) as it:
                norm_stats(nc, v, S, hx(it), N, it)
                norm_apply(nc, v, S, hx(it), N, xc, xn, it)
                if again:
                    v.wait_ge(S["normed"], it * W + W)
                    norm_stats(nc, v, S2, lambda w: xn[:, w], N2, it)
                    norm_apply(nc, v, S2, lambda w: xn[:, w], N2, xc, x2, it)
                for w in range(W):
                    v.wait_ge(S["logit_ps"], it * W + w + 1)
                    nc.vector.tensor_tensor(t.logit[:, w * G4:(w + 1) * G4, :],
                                            PS[w][:, 1, 0:G4 * E8].rearrange("p (g e) -> p g e", e=E8),
                                            bcast(C[pre + "_br"], 1, G4), ALU.add).then_inc(S["logit"], 1)
                v.wait_ge(S["logit"], it * W + W)
                nc.vector.tensor_reduce(t.m[:], t.logit[:], AX, ALU.max).then_inc(S["top"], 1)
                v.wait_ge(S["top"], it + 1)
                nc.vector.tensor_tensor(t.e[:], t.logit[:], bcast(t.m[:], 2, E8), ALU.subtract).then_inc(S["shifted"], 1)
                v.wait_ge(S["exp"], it + 1)
                if again:
                    gate_top2(nc, v, S, it, t.logit[:], t.e[:], C["prio"], t)
                else:
                    nc.vector.tensor_reduce(t.m[:], t.e[:], AX, ALU.add).then_inc(S["soft"], 1)
                    v.wait_ge(S["soft"], it * 3 + 1)
                    nc.vector.reciprocal(t.m[:], t.m[:]).then_inc(S["soft"], 1)
                    v.wait_ge(S["soft"], it * 3 + 2)
                    nc.vector.tensor_tensor(t.e[:], t.e[:], bcast(t.m[:], 2, E8), ALU.mult).then_inc(S["soft"], 1)
                    v.wait_ge(S["soft"], it * 3 + 3)
                    gate_top2(nc, v, S, it, t.e[:], t.e[:], C["prio"], t)
                ge = lambda ap: ap.rearrange("p (w g) e -> p w (g e)", w=W)
                split_bf16(nc, v, ge(t.w[:]), [parts[:, :, k, :] for k in range(PARTS)], [ge(b[:]) for b in t_b],
                           rest[:], S["parts"], it * 6)
                for w in range(W):
                    v.wait_ge(S["gT_ps"], it * W + w + 1)
                    nc.vector.tensor_tensor(gT[:, w].rearrange("p (g q) -> p g q", g=G4),
                                            bcast(PS[w][0:GR, 0, 0:P], 1, G4), bcast(C["gmask"][0:GR, :], 2, P),
                                            ALU.mult).then_inc(S["gT"], 1)
                for i, (w, s) in enumerate(steps):
                    v.wait_ge(S["gelu"], it * n_steps + i + 1)
                    v.wait_ge(S["gate_ps"], it * n_steps + i + 1)
                    if i >= 2:
                        v.wait_ge(S["gw_read"], it * n_steps + i - 1)
                    nc.vector.tensor_tensor(gw[:, i % 2, :], g[:, i % 2, :], gate_bank[i % 3], ALU.mult)\
                        .then_inc(S["gw"], 1)
                    if s == 3 and w >= 1:
                        add_output(v, it, w - 1)
                add_output(v, it, W - 1)
                v.wait_ge(S["h_new"], it * W + W)

        @block.scalar
        def _(act):
            act.wait_ge(C.sem(pre), C.count(pre))
            nc.scalar.copy(sel[:], C[pre + "_sel"][0:GR, :]).then_inc(S["sel"], 1)
            with act.Fori(0, ITERS) as it:
                for w in range(W):
                    act.wait_ge(S["xT_ps"], it * W + w + 1)
                    if again:
                        nc.scalar.activation(xT[:, w], PS[w][:, 0, 0:T], ACT.Identity, bias=C[pre + "_beta"],
                                             scale=C[pre + "_gamma"]).then_inc(S["xT"], 1)
                    else:
                        nc.scalar.copy(xT[:, w], PS[w][:, 0, 0:T]).then_inc(S["xT"], 1)
                act.wait_ge(S["shifted"], it + 1)
                nc.scalar.activation(t.e[:], t.e[:], ACT.Exp).then_inc(S["exp"], 1)
                b1 = C[pre + "_b1"]
                for i, (w, s) in enumerate(steps):
                    act.wait_ge(S["hid_ps"], it * n_steps + i + 1)
                    if i >= 2:
                        act.wait_ge(S["gw"], it * n_steps + i - 1)
                    nc.scalar.activation(g[:, i % 2, :], hid_bank[i % 3], ACT.Gelu, bias=b1[:, s:s + 1])\
                        .then_inc(S["gelu"], 1)
                    if s == 1 and w >= 1:
                        copy_output(act, it, w - 1)
                copy_output(act, it, W - 1)

        @block.tensor
        def _(pe):
            ident = C["ident"]
            w1 = C[pre + "_w1"].rearrange("p (s h n) -> p s h n", s=SL, h=2)
            w2 = C[pre + "_w2"].rearrange("p (s f) -> p s f", s=SL)

            def hidden(it, i):
                w, s = steps[i]
                if i >= 3:
                    pe.wait_ge(S["gelu"], it * n_steps + i - 2)
                for half in range(2):
                    ins = nc.tensor.matmul(hid_bank[i % 3][:, half * T:(half + 1) * T], w1[:, s, half, :], xT[:, w],
                                           start=True, stop=True)
                ins.then_inc(S["hid_ps"], 1)
                if i >= 3:
                    pe.wait_ge(S["gw"], it * n_steps + i - 2)
                nc.tensor.matmul(gate_bank[i % 3], sel[:, s * P:(s + 1) * P], gT[:, w], start=True, stop=True)\
                    .then_inc(S["gate_ps"], 1)

            def output(it, i):
                w, s = steps[i]
                y = y_bank[w % 2][0:D, :]
                if s == 0:
                    if w >= 2:
                        pe.wait_ge(S["h_new"], it * W + w - 1)
                    for k in range(PARTS):
                        nc.tensor.matmul(y, b2b[:, k, :], gT[:, w], start=(k == 0), stop=False)
                pe.wait_ge(S["gw"], it * n_steps + i + 1)
                nc.tensor.matmul(y, w2[:, s, :], gw[:, i % 2, :], start=False, stop=(s == SL - 1))\
                    .then_inc(S["gw_read"], 1)

            def turn_output(it, w):
                pe.wait_ge(C.sem("base"), C.count("base"))
                pe.wait_ge(S["yT"], it * W + w + 1)
                for k in range(G4):
                    at = (k % 2) * T + (k // 2) * P
                    ins = nc.tensor.transpose(y_bank[w % 2][:, k * D:(k + 1) * D], yT[:, w, at:at + P],
                                              ident[0:D, 0:D])
                ins.then_inc(S["y_ps"], 1)

            pe.wait_ge(C.sem(pre), C.count(pre))
            pe.wait_ge(S["sel"], 1)
            pe.wait_ge(S["b2"], 1)
            with pe.Fori(0, ITERS) as it:
                for w in range(W):
                    pe.wait_ge(S2["normed"], it * W + w + 1)
                    for u in range(U):
                        ins = nc.tensor.transpose(PS[w][:, 0, u * P:(u + 1) * P],
                                                  x2[:, w, 2 * u:2 * u + 2, :].rearrange("p g f -> p (g f)"), ident)
                    ins.then_inc(S["xT_ps"], 1)
                for w in range(W):
                    pe.wait_ge(S["xT"], it * W + w + 1)
                    for u in range(U):
                        at = u * 2 * E8
                        ins = nc.tensor.matmul(PS[w][:, 1, at:at + 2 * E8], xT[:, w, u * P:(u + 1) * P],
                                               C[pre + "_router"], start=True, stop=True)
                    ins.then_inc(S["logit_ps"], 1)
                pe.wait_ge(C.sem("base"), C.count("base"))
                pe.wait_ge(S["parts"], it * 6 + 6)
                for w in range(W):
                    nc.tensor.transpose(PS[w][0:GR, 0, 0:P], parts[:, w].rearrange("p k n -> p (k n)"), ident)\
                        .then_inc(S["gT_ps"], 1)
                pe.wait_ge(S["gT"], it * W + W)
                hidden(it, 0)
                hidden(it, 1)
                for i, (w, s) in enumerate(steps):
                    if i + 2 < n_steps:
                        hidden(it, i + 2)
                    output(it, i)
                    if s == 2 and w >= 1:
                        turn_output(it, w - 1)
                turn_output(it, W - 1)
                pe.wait_ge(S["h_new"], it * W + W)


def gelu_moe_128(nc, H, PS, C, dram):
    gelu_moe(nc, H, PS, C, dram, "m1", 128, True)



HEADS = 4
GROUPS6 = HEADS + 2
ROPE = 16
PLAIN = D - ROPE
WIN = 16
BLK = 32
BLOCKS = T // BLK
SPAN = WIN + BLK
DV = D + ROPE
RMS_EPS = 1e-8


def window_attention(nc, H, PS, C, dram):
    with ExitStack() as ctx:
        S = semaphores(nc, "win",
                        "zeros ms rms roped v pv_ps1 tables masks mixed_ps mixed squares square_sums rmsed "
                        "rope_terms qT_ps qT score_ps top shifted exp total inv prob probT_ps0 probT_ps1 "
                        "probT_low0 probT_low1 pv_ps0 outT0 outT1 y_ps h_new xT_ps xT kv_ps kv q_ps kT_ps kT "
                        "probT_high0 probT_high1 edgeT_ps edgeT yT_ps yT")
        sb = lambda name, shape, dt=F32: ctx.enter_context(nc.sbuf_tensor("win_" + name, shape, dt))
        N = NormBuffers(nc, ctx, "win")
        x_or_y = sb("x_or_y", [P, 2 * W * G4 * D])
        xc, xn = (t.rearrange("p (w g f) -> p w g f", w=W, g=G4) for t in (x_or_y[:, 0:W * CW], x_or_y[:, W * CW:]))
        yT = x_or_y[0:D, :].rearrange("p (w n) -> p w n", w=W)
        xT = sb("xT", [P, W, T])
        TILE = HEADS * P
        big = sb("big", [P, W, (G4 + 1) * TILE])
        qkv = [big[:, w, 0:U * GROUPS6 * P].rearrange("p (u j n) -> p u j n", u=U, j=GROUPS6) for w in range(W)]
        probT = [big[:, w, 0:G4 * TILE].rearrange("p (g n) -> p g n", g=G4) for w in range(W)]
        edgeT = [big[:, w, G4 * TILE:G4 * TILE + 2 * P].rearrange("p (h n) -> p h n", h=2) for w in range(W)]
        out = sb("out", [P, W, HEADS * 2 * T])
        squares = [out[:, w, 0:U * GROUPS6 * P].rearrange("p (u j h f) -> p u j h f", u=U, j=GROUPS6, h=2)
                   for w in range(W)]
        outT = [out[0:DV, w, :].rearrange("p (j n) -> p j n", j=HEADS) for w in range(W)]
        ms = sb("ms", [P, W, U, GROUPS6, 2])
        rms = sb("rms", [P, W, U, GROUPS6, 2])
        minus_half = sb("minus_half", [P, W * U * GROUPS6 * 2])
        cosw, sinw = sb("cosw", [P, U, GROUPS6, ROPE]), sb("sinw", [P, U, GROUPS6, ROPE])
        terms = sb("terms", [P, 2 * W * U * GROUPS6 * 2 * ROPE])
        ra, rb = (terms[:, k * W * U * GROUPS6 * 2 * ROPE:(k + 1) * W * U * GROUPS6 * 2 * ROPE]
                  .rearrange("p (w k h f) -> p w k h f", w=W, h=2, f=ROPE) for k in range(2))
        e = terms[:].rearrange("p (w b k) -> p w b k", w=W, k=SPAN)
        v = sb("v", [P, W, U, 2, DV])
        qT = sb("qT", [P, W, BLOCKS, HEADS, BLK])
        kT = sb("kT", [P, W, WIN + T])
        top, total = sb("top", [P, W, 2 * BLOCKS]), sb("total", [P, W, 2 * BLOCKS])
        prob = sb("prob", [P, W, 2 * BLOCKS, P])
        edge = sb("edge", [P, W, 2, P])
        maskb = sb("maskb", [P, BLOCKS * SPAN], BF16)
        identb = sb("identb", [P, P], BF16)
        wqk = sb("wqk", [P, HEADS])
        mixed = sb("mixed", [DV, HEADS, D])
        obias = sb("obias", [D, 1])
        block = ctx.enter_context(nc.Block())
        hx = lambda it: (lambda w: groups(chunk_of(H, it, w)))
        even, odd = slice(0, ROPE, 2), slice(1, ROPE, 2)

        @block.sync
        def _(sp):
            C.load(sp, "m2")

        @block.gpsimd
        def _(pool):
            pool.wait_ge(C.sem("win"), C.count("win"))
            nc.gpsimd.memset(prob[:], 0.0).then_inc(S["zeros"], 1)
            nc.gpsimd.memset(edge[:], 0.0).then_inc(S["zeros"], 1)
            nc.gpsimd.memset(kT[:], 0.0).then_inc(S["zeros"], 1)
            nc.gpsimd.memset(minus_half[:], -0.5).then_inc(S["zeros"], 1)
            with pool.Fori(0, ITERS) as it:
                norm_rstd(nc, pool, S, C, N, it)
                pool.wait_ge(S["zeros"], 4)
                pool.wait_ge(S["ms"], it + 1)
                nc.gpsimd.tensor_tensor(rms[:].rearrange("p w u j h -> p (w u j h)"),
                                        ms[:].rearrange("p w u j h -> p (w u j h)"), minus_half[:], ALU.pow)\
                    .then_inc(S["rms"], 1)
                for w in range(W):
                    pool.wait_ge(S["roped"], it * W + w + 1)
                    src = qkv[w][:, :, HEADS + 1, :].rearrange("p u (h f) -> p u h f", h=2)
                    gain = C["win_wv"].unsqueeze(1).unsqueeze(1).broadcast_to([P, U, 2, D])
                    nc.gpsimd.tensor_tensor(v[:, w, :, :, 0:D], src, gain, ALU.mult)
                    nc.gpsimd.tensor_copy(v[:, w, :, :, D:DV:2], src[:, :, :, PLAIN + 1:D:2])
                    nc.gpsimd.tensor_copy(v[:, w, :, :, D + 1:DV:2], src[:, :, :, PLAIN:D:2]).then_inc(S["v"], 1)
                pool.wait_ge(S["pv_ps1"], it * W + W)

        @block.vector
        def _(vec):
            vec.wait_ge(C.sem("win"), C.count("win"))
            rope3 = lambda ap: ap.rearrange("p (u j f) -> p u j f", u=U, j=GROUPS6)
            nc.vector.tensor_tensor(cosw[:], rope3(C["win_cos"]), bcast(C["win_w"].rearrange("p (j f) -> p j f", f=ROPE), 1, U),
                                    ALU.mult).then_inc(S["tables"], 1)
            nc.vector.tensor_tensor(sinw[:], rope3(C["win_sin"]), bcast(C["win_ws"].rearrange("p (j f) -> p j f", f=ROPE), 1, U),
                                    ALU.mult).then_inc(S["tables"], 1)
            nc.vector.tensor_tensor(wqk[:], C["win_wqT"], C["win_wkT"].broadcast_to([P, HEADS]), ALU.mult)\
                .then_inc(S["tables"], 1)
            nc.vector.tensor_copy(maskb[:], C["win_mask"]).then_inc(S["masks"], 1)
            nc.vector.tensor_copy(identb[:], C["ident"]).then_inc(S["masks"], 1)
            vec.wait_ge(S["mixed_ps"], 1)
            nc.vector.tensor_copy(mixed[:].rearrange("p j d -> p (j d)"), PS[0][0:DV, 0, 0:HEADS * D])\
                .then_inc(S["mixed"], 1)
            nc.vector.tensor_tensor(obias[:], PS[0][0:D, 1, 0:1], C["win_bout"][0:D, :], ALU.add).then_inc(S["mixed"], 1)
            vec.wait_ge(S["zeros"], 4)
            vec.wait_ge(S["tables"], 3)
            with vec.Fori(0, ITERS) as it:
                norm_stats(nc, vec, S, hx(it), N, it)
                norm_apply(nc, vec, S, hx(it), N, xc, xn, it)
                for w in range(W):
                    vec.wait_ge(S["squares"], it * W + w + 1)
                    nc.vector.tensor_reduce(ms[:, w], squares[w], AX, ALU.add).then_inc(S["square_sums"], 1)
                vec.wait_ge(S["square_sums"], it * W + W)
                nc.vector.tensor_scalar(ms[:], ms[:], 1.0 / D, RMS_EPS, ALU.mult, ALU.add).then_inc(S["ms"], 1)
                vec.wait_ge(S["rms"], it + 1)
                for w in range(W):
                    for u in range(U):
                        x = qkv[w][:, u, 0:HEADS, :].rearrange("p j (h f) -> p (j h) f", h=2)
                        scale = bcast(rms[:, w, u, 0:HEADS, :].rearrange("p j h -> p (j h)"), 2, D)
                        nc.vector.tensor_tensor(x, PS[w][:, u, :].rearrange("p (k f) -> p k f", f=D), scale, ALU.mult)
                        x = qkv[w][:, u, HEADS:, :].rearrange("p j (h f) -> p (j h) f", h=2)
                        scale = bcast(rms[:, w, u, HEADS:, :].rearrange("p j h -> p (j h)"), 2, D)
                        ins = nc.vector.tensor_tensor(x, x, scale, ALU.mult)
                    ins.then_inc(S["rmsed"], 1)
                for w in range(W):
                    vec.wait_ge(S["rmsed"], it * W + w + 1)
                    x = qkv[w].rearrange("p u j (h f) -> p (u j) h f", h=2)[:, :, :, PLAIN:]
                    cosb = bcast(cosw[:].rearrange("p u j f -> p (u j) f"), 2, 2)
                    sinb = bcast(sinw[:].rearrange("p u j f -> p (u j) f"), 2, 2)
                    nc.vector.tensor_tensor(ra[:, w], x, cosb, ALU.mult)
                    nc.vector.tensor_tensor(rb[:, w, :, :, even], x[:, :, :, odd], sinb[:, :, :, even], ALU.mult)
                    nc.vector.tensor_tensor(rb[:, w, :, :, odd], x[:, :, :, even], sinb[:, :, :, odd], ALU.mult)\
                        .then_inc(S["rope_terms"], 1)
                for w in range(W):
                    vec.wait_ge(S["rope_terms"], it * W + w + 1)
                    x = qkv[w].rearrange("p u j (h f) -> p (u j) h f", h=2)[:, :, :, PLAIN:]
                    nc.vector.tensor_tensor(x, ra[:, w], rb[:, w], ALU.add).then_inc(S["roped"], 1)
                for w in range(W):
                    vec.wait_ge(S["qT_ps"], it * W + w + 1)
                    for u in range(U):
                        dst = qT[:, w, u * (BLOCKS // U):(u + 1) * (BLOCKS // U)].rearrange("p b j q -> p j b q")
                        ins = nc.vector.tensor_tensor(
                            dst, PS[w][:, u, :].rearrange("p (j b q) -> p j b q", j=HEADS, q=BLK),
                            wqk[:].unsqueeze(2).unsqueeze(3).broadcast_to([P, HEADS, BLOCKS // U, BLK]), ALU.mult)
                    ins.then_inc(S["qT"], 1)
                for w in range(W):
                    vec.wait_ge(S["score_ps"], it * W + w + 1)
                    for half in range(2):
                        at = slice(half * BLOCKS, (half + 1) * BLOCKS)
                        s = PS[w][:, half, 0:BLOCKS * SPAN].rearrange("p (b k) -> p b k", k=SPAN)
                        ins = nc.vector.tensor_reduce(top[:, w, at], s, AX, ALU.max)
                    ins.then_inc(S["top"], 1)
                for w in range(W):
                    vec.wait_ge(S["top"], it * W + w + 1)
                    for half in range(2):
                        at = slice(half * BLOCKS, (half + 1) * BLOCKS)
                        s = PS[w][:, half, 0:BLOCKS * SPAN].rearrange("p (b k) -> p b k", k=SPAN)
                        ins = nc.vector.tensor_tensor(e[:, w, at], s, bcast(top[:, w, at], 2, SPAN), ALU.subtract)
                    ins.then_inc(S["shifted"], 1)
                for w in range(W):
                    vec.wait_ge(S["exp"], it * W + w + 1)
                    nc.vector.tensor_reduce(total[:, w], e[:, w], AX, ALU.add).then_inc(S["total"], 1)
                for w in range(W):
                    vec.wait_ge(S["total"], it * W + w + 1)
                    nc.vector.reciprocal(total[:, w], total[:, w]).then_inc(S["inv"], 1)
                for w in range(W):
                    vec.wait_ge(S["inv"], it * W + w + 1)
                    nb = BLOCKS // U
                    for g in range(G4):
                        b0 = g * nb
                        dst = prob[:, w, b0:b0 + nb, :].rearrange("p b k -> p (b k)")[:, P + BLK - WIN:]
                        step = P + BLK
                        dst = diagonal(dst, nb - 1, step, SPAN)
                        nc.vector.tensor_tensor(dst, e[:, w, b0 + 1:b0 + nb, :], bcast(total[:, w, b0 + 1:b0 + nb], 2, SPAN),
                                                ALU.mult)
                    own = prob[:, w].rearrange("p (g b) k -> p g b k", b=nb)[:, :, 0, 0:BLK]
                    src = e[:, w].rearrange("p (g b) k -> p g b k", b=nb)[:, :, 0, :]
                    inv = total[:, w].rearrange("p (g b) -> p g b", b=nb)[:, :, 0]
                    nc.vector.tensor_tensor(own, src[:, :, WIN:], bcast(inv, 2, BLK), ALU.mult)
                    nc.vector.tensor_tensor(edge[:, w, :, P - WIN:], src[:, 1::2, 0:WIN], bcast(inv[:, 1::2], 2, WIN),
                                            ALU.mult).then_inc(S["prob"], 1)
                for half in range(2):
                    for w in range(W):
                        vec.wait_ge(S["v"], it * W + w + 1)
                        vec.wait_ge(S["probT_ps0"] if half == 0 else S["probT_ps1"], it * W + w + 1)
                        nc.vector.tensor_copy(probT[w][:, 2 * half, :], PS[w][:, 0, :])\
                            .then_inc(S["probT_low0"] if half == 0 else S["probT_low1"], 1)
                for half in range(2):
                    for w in range(W):
                        vec.wait_ge(S["pv_ps0"] if half == 0 else S["pv_ps1"], it * W + w + 1)
                        for u in range(U):
                            nb = BLOCKS // U
                            at = (half * U + u) * P
                            dst = outT[w][:, :, at:at + P].rearrange("p j (b q) -> p b j q", q=BLK)
                            rot = C["win_turn"][0:DV, u * P:(u + 1) * P].rearrange("p (b q) -> p b q", q=BLK)
                            ins = nc.vector.tensor_tensor(
                                dst, PS[w][0:DV, u, :].rearrange("p (b j q) -> p b j q", b=nb, j=HEADS),
                                bcast(rot, 2, HEADS), ALU.mult)
                        ins.then_inc(S["outT0"] if half == 0 else S["outT1"], 1)
                for w in range(W):
                    vec.wait_ge(S["y_ps"], it * W + w + 1)
                    x = hx(it)(w)
                    nc.vector.tensor_tensor(x, x, groups(PS[w][:, 1, 0:CW]), ALU.add).then_inc(S["h_new"], 1)
                vec.wait_ge(S["h_new"], it * W + W)

        @block.scalar
        def _(act):
            act.wait_ge(C.sem("win"), C.count("win"))
            act.wait_ge(S["zeros"], 4)
            act.wait_ge(S["mixed"], 2)
            with act.Fori(0, ITERS) as it:
                for w in range(W):
                    act.wait_ge(S["xT_ps"], it * W + w + 1)
                    nc.scalar.copy(xT[:, w], PS[w][:, 0, 0:T]).then_inc(S["xT"], 1)
                for w in range(W):
                    act.wait_ge(S["kv_ps"], it * W + w + 1)
                    kv = PS[w][:, 0, :].rearrange("p (u n) -> p u n", u=U)
                    dst = lambda t: t[:, :, HEADS:, :].rearrange("p u j n -> p u (j n)")
                    nc.scalar.copy(dst(qkv[w]), kv)
                    nc.scalar.activation(out[:, w, 0:U * GROUPS6 * P].rearrange("p (u n) -> p u n", u=U)[:, :, HEADS * P:],
                                         kv, ACT.Square).then_inc(S["kv"], 1)
                for w in range(W):
                    act.wait_ge(S["q_ps"], it * W + w + 1)
                    for u in range(U):
                        at = u * GROUPS6 * P
                        ins = nc.scalar.activation(out[:, w, at:at + HEADS * P], PS[w][:, u, :], ACT.Square)
                    ins.then_inc(S["squares"], 1)
                for w in range(W):
                    act.wait_ge(S["kT_ps"], it * W + w + 1)
                    nc.scalar.copy(kT[:, w, WIN:], PS[w][:, 0, 0:T]).then_inc(S["kT"], 1)
                for w in range(W):
                    act.wait_ge(S["shifted"], it * W + w + 1)
                    nc.scalar.activation(e[:, w], e[:, w], ACT.Exp, scale=D ** -0.5).then_inc(S["exp"], 1)
                for half in range(2):
                    for w in range(W):
                        act.wait_ge(S["v"], it * W + w + 1)
                        act.wait_ge(S["probT_ps0"] if half == 0 else S["probT_ps1"], it * W + w + 1)
                        nc.scalar.copy(probT[w][:, 2 * half + 1, :], PS[w][:, 1, :])\
                            .then_inc(S["probT_high0"] if half == 0 else S["probT_high1"], 1)
                for w in range(W):
                    act.wait_ge(S["edgeT_ps"], it * W + w + 1)
                    nc.scalar.copy(edgeT[w], PS[w][:, 0, 0:2 * P].rearrange("p (h n) -> p h n", h=2)).then_inc(S["edgeT"], 1)
                for w in range(W):
                    act.wait_ge(S["yT_ps"], it * W + w + 1)
                    nc.scalar.activation(yT[:, w], PS[w][0:D, 0, :], ACT.Identity, bias=obias[:]).then_inc(S["yT"], 1)

        @block.tensor
        def _(pe):
            ident = C["ident"]
            wgt = C["win_qkv"].rearrange("p (j n) -> p j n", j=GROUPS6)
            nb = BLOCKS // U
            pe.wait_ge(C.sem("win"), C.count("win"))
            for j in range(HEADS):
                nc.tensor.matmul(PS[0][0:DV, 0, j * D:(j + 1) * D], C["win_wg"][0:D, j * DV:(j + 1) * DV],
                                 C["win_wo"][0:D, (j // 2) * D:(j // 2 + 1) * D], start=True, stop=True)
            nc.tensor.matmul(PS[0][0:D, 1, 0:1], C["win_wo2"], C["win_bg"], start=True, stop=True).then_inc(S["mixed_ps"], 1)
            pe.wait_ge(S["mixed"], 2)
            pe.wait_ge(S["masks"], 2)
            with pe.Fori(0, ITERS) as it:
                for w in range(W):
                    pe.wait_ge(S["normed"], it * W + w + 1)
                    for u in range(U):
                        ins = nc.tensor.transpose(PS[w][:, 0, u * P:(u + 1) * P],
                                                  xn[:, w, 2 * u:2 * u + 2, :].rearrange("p g f -> p (g f)"), ident)
                    ins.then_inc(S["xT_ps"], 1)
                for w in range(W):
                    pe.wait_ge(S["xT"], it * W + w + 1)
                    for u in range(U):
                        ins = nc.tensor.matmul(PS[w][:, 0, u * 2 * P:(u + 1) * 2 * P], xT[:, w, u * P:(u + 1) * P],
                                               wgt[:, HEADS:, :].rearrange("p j n -> p (j n)"), start=True, stop=True)
                    ins.then_inc(S["kv_ps"], 1)
                for w in range(W):
                    pe.wait_ge(S["kv"], it * W + w + 1)
                    for u in range(U):
                        ins = nc.tensor.matmul(PS[w][:, u, :], xT[:, w, u * P:(u + 1) * P],
                                               wgt[:, 0:HEADS, :].rearrange("p j n -> p (j n)"), start=True, stop=True)
                    ins.then_inc(S["q_ps"], 1)
                for w in range(W):
                    pe.wait_ge(S["roped"], it * W + w + 1)
                    for u in range(U):
                        for j in range(HEADS):
                            ins = nc.tensor.transpose(PS[w][:, u, j * P:(j + 1) * P], qkv[w][:, u, j, :], ident)
                    ins.then_inc(S["qT_ps"], 1)
                for w in range(W):
                    pe.wait_ge(S["qT"], it * W + w + 1)
                    for u in range(U):
                        ins = nc.tensor.transpose(PS[w][:, 0, u * P:(u + 1) * P], qkv[w][:, u, HEADS, :], ident)
                    ins.then_inc(S["kT_ps"], 1)
                for w in range(W):
                    pe.wait_ge(S["kT"], it * W + w + 1)
                    for half in range(2):
                        rows = slice(half * D, (half + 1) * D)
                        nc.tensor.matmul(PS[w][:, half, 0:BLOCKS * SPAN], identb[:], maskb[:], start=True, stop=False)
                        for b in range(BLOCKS):
                            ins = nc.tensor.matmul(PS[w][:, half, b * SPAN:(b + 1) * SPAN],
                                                   qT[rows, w, b].rearrange("p j q -> p (j q)"),
                                                   kT[rows, w, b * BLK:b * BLK + SPAN], start=False, stop=(b == BLOCKS - 1))
                    ins.then_inc(S["score_ps"], 1)
                for half in range(2):
                    for w in range(W):
                        pe.wait_ge(S["prob"], it * W + w + 1)
                        if half == 1:
                            pe.wait_ge(S["probT_low0"], it * W + w + 1)
                            pe.wait_ge(S["probT_high0"], it * W + w + 1)
                        for u in range(U):
                            for b in range(nb):
                                ins = nc.tensor.transpose(PS[w][:, u, b * P:(b + 1) * P],
                                                          prob[:, w, half * BLOCKS + u * nb + b, :], ident)
                        ins.then_inc(S["probT_ps0"] if half == 0 else S["probT_ps1"], 1)
                for w in range(W):
                    pe.wait_ge(S["probT_low1"], it * W + w + 1)
                    for half in range(2):
                        ins = nc.tensor.transpose(PS[w][:, 0, half * P:(half + 1) * P], edge[:, w, half, :], ident)
                    ins.then_inc(S["edgeT_ps"], 1)
                for half in range(2):
                    for w in range(W):
                        pe.wait_ge(S["v"], it * W + w + 1)
                        pe.wait_ge(S["edgeT"], it * W + w + 1)
                        pe.wait_ge(S["probT_high1"], it * W + w + 1)
                        if half == 1:
                            pe.wait_ge(S["outT0"], it * W + w + 1)
                        for u in range(U):
                            ins = nc.tensor.matmul(PS[w][0:DV, u, :], v[:, w, u, half, :], probT[w][:, half * U + u, :],
                                                   start=True, stop=(u == 0))
                        ins = nc.tensor.matmul(PS[w][0:DV, 1, 0:P], v[:, w, 0, half, :], edgeT[w][:, half, :],
                                               start=False, stop=True)
                        ins.then_inc(S["pv_ps0"] if half == 0 else S["pv_ps1"], 1)
                for w in range(W):
                    pe.wait_ge(S["outT1"], it * W + w + 1)
                    for j in range(HEADS):
                        ins = nc.tensor.matmul(PS[w][0:D, 0, :], mixed[:, j, :], outT[w][:, j, :], start=(j == 0),
                                               stop=(j == HEADS - 1))
                    ins.then_inc(S["yT_ps"], 1)
                for w in range(W):
                    pe.wait_ge(C.sem("base"), C.count("base"))
                    pe.wait_ge(S["yT"], it * W + w + 1)
                    for g in range(G4):
                        at = (g % 2) * T + (g // 2) * P
                        ins = nc.tensor.transpose(PS[w][:, 1, g * D:(g + 1) * D], yT[:, w, at:at + P],
                                                  ident[0:D, 0:D])
                    ins.then_inc(S["y_ps"], 1)


def gelu_moe_64(nc, H, PS, C, dram):
    gelu_moe(nc, H, PS, C, dram, "m2", 64, False)



ORDER = 8
TAPS = ORDER + 1
LT = T // 2
PAIRS = D // 2
STEP = 256
STEPS = D * D // STEP
RSTEPS = STEPS // ITERS
assert RSTEPS == 2 * W


def rational_convolution(nc, H, PS, C, dram):
    with ExitStack() as ctx:
        S = semaphores(nc, "rat",
                        "den num nyqT ht ht_row zeros sq inv q terms sums nyq coef coef_ps xf_ps hf_ps hf_even "
                        "hf_odd ends prod_ps prod_even prodT_ps x1 Y out_ps h_new nyq_ps xf prod_odd")
        sb = lambda name, shape, dt=F32: ctx.enter_context(nc.sbuf_tensor("rat_" + name, shape, dt))
        N = NormBuffers(nc, ctx, "rat")
        xd = sb("xd", [P, W, G4, 2, D])
        ht = sb("ht", [P, 2, D * D])
        prod = ht[:].rearrange("p c n -> p (c n)").rearrange("p (n l) -> p n l", l=LT)
        xf = sb("xf", [P, 2, LT, 2, 2, B])
        hf = sb("hf", [P, 2 * LT * 2 * PAIRS])
        resp = hf[:].rearrange("p (t l c m) -> p t l c m", t=2, l=LT, c=2)
        at = [0]

        def part(n):
            at[0] += n
            return hf[:, at[0] - n:at[0]]

        den = part(D * D)[0:TAPS, :]
        num = part(D * D)[0:2 * TAPS, :]
        dens, sq, direct, cross, sums = (part(2 * 2 * STEP).rearrange("p (s c n) -> p s c n", s=2, c=2) for _ in range(5))
        q, inv = (part(2 * STEP).rearrange("p (s n) -> p s n", s=2) for _ in range(2))
        xc = part(W * CW).rearrange("p (w g f) -> p w g f", w=W, g=G4)
        nyq_terms = part(2 * PAIRS * TAPS).rearrange("p (a m k) -> p a m k", a=2, m=PAIRS)
        Y = hf[:, 0:4 * D * B].rearrange("p (t c n) -> p t c n", t=2, c=2)
        x1 = hf[:, 4 * D * B:4 * D * B + 2 * 4 * P].rearrange("p (s m c t n) -> p s m c t n", s=4, m=2, c=2, t=2)
        ends = sb("ends", [P, 2, 2, PAIRS])
        nyq = sb("nyq", [P, 2, PAIRS])
        nyqT = sb("nyqT", [PAIRS, P])
        banks = [PS[k // 2][:, k % 2, :] for k in range(2 * W)]
        block = ctx.enter_context(nc.Block())
        hx = lambda it: (lambda w: groups(chunk_of(H, it, w)))

        @block.sync
        def _(sp):
            sp.dma_start(den, dram["rat_den"]).then_inc(S["den"], 16)
            sp.dma_start(num, dram["rat_num"]).then_inc(S["num"], 16)
            C.load(sp, "dep")
            sp.wait_ge(S["nyqT"], 1)
            sp.wait_ge(S["ht"], STEPS)
            sp.dma_start(ht[0:1, 1, :].rearrange("o (m q) -> o m q", q=P), nyqT[:]).then_inc(S["ht_row"], 16)
            sp.wait_ge(S["ht_row"], 16)

        @block.gpsimd
        def _(pool):
            nc.gpsimd.memset(xf[:], 0.0).then_inc(S["zeros"], 1)
            nc.gpsimd.memset(ends[:], 0.0).then_inc(S["zeros"], 1)
            with pool.Fori(0, ITERS) as it:
                norm_rstd(nc, pool, S, C, N, it)
                for s in range(RSTEPS):
                    k = s % 2
                    pool.wait_ge(S["sq"], it * RSTEPS + s + 1)
                    if s >= 2:
                        pool.wait_ge(S["inv"], it * RSTEPS + s - 1)
                    nc.gpsimd.tensor_tensor(q[:, k], sq[:, k, 0], sq[:, k, 1], ALU.add).then_inc(S["q"], 1)
                    pool.wait_ge(S["terms"], it * RSTEPS + s + 1)
                    if s >= 2:
                        pool.wait_ge(S["ht"], it * RSTEPS + s - 1)
                    nc.gpsimd.tensor_tensor(sums[:, k, 0], direct[:, k, 0], direct[:, k, 1], ALU.add)
                    nc.gpsimd.tensor_tensor(sums[:, k, 1], cross[:, k, 0], cross[:, k, 1], ALU.subtract)\
                        .then_inc(S["sums"], 1)
                pool.wait_ge(S["inv"], it * RSTEPS + RSTEPS)
                pool.wait_ge(S["ht"], it * RSTEPS + RSTEPS)

        @block.vector
        def _(v):
            v.wait_ge(C.sem("rat"), C.count("rat"))
            signs = bcast(C["rat_signs"], 1, PAIRS)
            for a in range(2):
                nc.vector.tensor_tensor(nyq_terms[:, a], C[("rat_b", "rat_a")[a]].rearrange("p (m k) -> p m k", k=TAPS),
                                        signs, ALU.mult).then_inc(S["nyq"], 1)
            v.wait_ge(S["nyq"], 2)
            for a in range(2):
                nc.vector.tensor_reduce(nyq[:, a], nyq_terms[:, a], AX, ALU.add).then_inc(S["nyq"], 1)
            v.wait_ge(S["nyq"], 4)
            nc.vector.reciprocal(nyq[:, 1], nyq[:, 1]).then_inc(S["nyq"], 1)
            v.wait_ge(S["nyq"], 5)
            nc.vector.tensor_tensor(nyq[:, 0], nyq[:, 0], nyq[:, 1], ALU.mult).then_inc(S["nyq"], 1)
            v.wait_ge(S["nyq"], 6)
            nc.vector.tensor_tensor(nyq[:, 0], nyq[:, 0], C["rat_h0"], ALU.add).then_inc(S["nyq"], 1)
            v.wait_ge(S["den"], 16)
            v.wait_ge(S["num"], 16)
            nc.vector.tensor_tensor(num[0:TAPS, :], num[0:TAPS, :], den, ALU.mult).then_inc(S["coef"], 1)

            def finish(it, s):
                k = s % 2
                v.wait_ge(S["inv"], it * RSTEPS + s + 1)
                v.wait_ge(S["sums"], it * RSTEPS + s + 1)
                nc.vector.tensor_tensor(ht[:, :, bass.ds(it * (RSTEPS * STEP) + s * STEP, STEP)], sums[:, k],
                                        bcast(inv[:, k], 1, 2), ALU.mult).then_inc(S["ht"], 1)

            with v.Fori(0, ITERS) as it:
                norm_stats(nc, v, S, hx(it), N, it)
                for w in range(W):
                    nc.vector.tensor_tensor(xc[:, w], hx(it)(w), bcast(N.mean[:, w * G4:(w + 1) * G4], 2, D),
                                            ALU.subtract).then_inc(S["norm_centred"], 1)
                for w in range(W):
                    v.wait_ge(S["norm_centred"], it * W + w + 1)
                    v.wait_ge(S["norm_rstd"], it + 1)
                    nc.vector.tensor_tensor(xd[:, w], bcast(xc[:, w], 2, 2),
                                            N.rstd[:, w * G4:(w + 1) * G4].unsqueeze(2).unsqueeze(3)
                                            .broadcast_to([P, G4, 2, D]), ALU.mult).then_inc(S["normed"], 1)
                for s in range(RSTEPS):
                    k = s % 2
                    n, d = PS[k][:, 0, :].rearrange("p (c n) -> p c n", c=2), dens[:, k]
                    v.wait_ge(S["coef_ps"], it * RSTEPS + s + 1)
                    v.wait_ge(S["sq"], it * RSTEPS + s + 1)
                    if s >= 2:
                        v.wait_ge(S["sums"], it * RSTEPS + s - 1)
                    nc.vector.tensor_tensor(direct[:, k], n, d, ALU.mult)
                    nc.vector.tensor_tensor(cross[:, k, 0], n[:, 1], d[:, 0], ALU.mult)
                    nc.vector.tensor_tensor(cross[:, k, 1], n[:, 0], d[:, 1], ALU.mult).then_inc(S["terms"], 1)
                    if s:
                        finish(it, s - 1)
                    v.wait_ge(S["q"], it * RSTEPS + s + 1)
                    nc.vector.reciprocal(inv[:, k], q[:, k]).then_inc(S["inv"], 1)
                finish(it, RSTEPS - 1)
                v.wait_ge(S["xf_ps"], it * RSTEPS + RSTEPS)
            v.wait_ge(S["zeros"], 2)
            with v.Fori(0, PAIRS // 8) as it:
                for r in range(4):
                    v.wait_ge(S["hf_ps"], it * 8 + 2 * r + 1)
                    dst = resp[:, :, :, :, bass.ds(it * 8 + 2 * r, 1)].rearrange("p t l c o -> p t c (l o)")
                    nc.vector.tensor_copy(dst, banks[2 * r].rearrange("p (t c l) -> p t c l", t=2, c=2))\
                        .then_inc(S["hf_even"], 1)
            v.wait_ge(S["hf_even"], PAIRS // 2)
            v.wait_ge(S["hf_odd"], PAIRS // 2)
            for c in range(2):
                nc.vector.tensor_copy(ends[:, c, 0, :], resp[:, 0, 0, c, :]).then_inc(S["ends"], 1)
            with v.Fori(0, LT // 8 // 8) as it:
                for r in range(4):
                    v.wait_ge(S["prod_ps"], it * 8 + 2 * r + 1)
                    nc.vector.tensor_copy(prod[:, :, bass.ds(it * 64 + 16 * r, 8)],
                                          banks[2 * r].rearrange("p (l n) -> p n l", l=8)).then_inc(S["prod_even"], 1)
            with v.Fori(0, PAIRS // 8) as it:
                for r in range(4):
                    v.wait_ge(S["prodT_ps"], it * 4 + r + 1)
                    v.wait_ge(S["x1"], it * 4 + r + 1)
                    pt = banks[r].rearrange("p (m c t x n) -> p c x m t n", m=2, c=2, t=2, x=2)
                    dst = lambda c: Y[:, :, c, bass.ds(it * (8 * 2 * B) + r * (4 * B), 4 * B)]\
                        .rearrange("p t (m n) -> p m t n", m=2)
                    nc.vector.tensor_tensor(dst(0), pt[:, 0, 0], x1[:, r, :, 1], ALU.subtract)
                    nc.vector.tensor_tensor(dst(1), pt[:, 1, 0], x1[:, r, :, 0], ALU.add).then_inc(S["Y"], 1)
            hv = H[:].rearrange("p (c u h f) -> p u h c f", c=CHUNKS, u=U, h=2)
            for k in range(2 * U):
                u, nh = k // 2, k % 2
                v.wait_ge(S["out_ps"], k + 1)
                x = hv[:, u, :, :, nh * PAIRS:(nh + 1) * PAIRS]
                nc.vector.tensor_tensor(x, x, banks[4 + k].rearrange("p (j h c) -> p h c j", h=2, c=CHUNKS), ALU.add)\
                    .then_inc(S["h_new"], 1)

        @block.scalar
        def _(act):
            act.wait_ge(S["nyq_ps"], 1)
            nc.scalar.copy(nyqT[:], banks[4][0:PAIRS, 0:P]).then_inc(S["nyqT"], 1)
            act.wait_ge(S["zeros"], 2)
            with act.Fori(0, ITERS) as it:
                for s in range(RSTEPS):
                    k = s % 2
                    act.wait_ge(S["coef_ps"], it * RSTEPS + s + 1)
                    if s >= 2:
                        act.wait_ge(S["q"], it * RSTEPS + s - 1)
                        act.wait_ge(S["terms"], it * RSTEPS + s - 1)
                    nc.scalar.copy(dens[:, k].rearrange("p c n -> p (c n)"), PS[k][:, 1, :])
                    nc.scalar.activation(sq[:, k].rearrange("p c n -> p (c n)"), PS[k][:, 1, :], ACT.Square)\
                        .then_inc(S["sq"], 1)
                    act.wait_ge(S["xf_ps"], it * RSTEPS + s + 1)
                    w, half = s // 2, s % 2
                    for j2 in range(2):
                        rows = slice(j2 * D, (j2 + 1) * D)
                        dst = xf[rows, :, :, :, j2, bass.ds(it * W + w + CHUNKS * half, 1)]\
                            .rearrange("p t l x o -> p t x (l o)")
                        ins = nc.scalar.copy(dst, banks[4 + s % 4][rows, :].rearrange("p (t x l) -> p t x l", t=2, x=2))
                    ins.then_inc(S["xf"], 1)
                act.wait_ge(S["q"], it * RSTEPS + RSTEPS)
                act.wait_ge(S["terms"], it * RSTEPS + RSTEPS)
            with act.Fori(0, PAIRS // 8) as it:
                for r in range(4):
                    act.wait_ge(S["hf_ps"], it * 8 + 2 * r + 2)
                    dst = resp[:, :, :, :, bass.ds(it * 8 + 2 * r + 1, 1)].rearrange("p t l c o -> p t c (l o)")
                    nc.scalar.copy(dst, banks[2 * r + 1].rearrange("p (t c l) -> p t c l", t=2, c=2))\
                        .then_inc(S["hf_odd"], 1)
            with act.Fori(0, LT // 8 // 8) as it:
                for r in range(4):
                    act.wait_ge(S["prod_ps"], it * 8 + 2 * r + 2)
                    nc.scalar.copy(prod[:, :, bass.ds(it * 64 + 16 * r + 8, 8)],
                                   banks[2 * r + 1].rearrange("p (l n) -> p n l", l=8)).then_inc(S["prod_odd"], 1)

            with act.Fori(0, PAIRS // 8) as it:
                for r in range(4):
                    act.wait_ge(S["prodT_ps"], it * 4 + r + 1)
                    nc.scalar.copy(x1[:, r].rearrange("p m c t n -> p (m c) t n"),
                                   banks[r].rearrange("p (mc t x n) -> p x mc t n", t=2, x=2, n=2 * B)[:, 1])\
                        .then_inc(S["x1"], 1)
                act.wait_ge(S["Y"], it * 4 + 4)

        @block.tensor
        def _(pe):
            ident = C["ident"]
            dft9 = C["rat_dft9"].rearrange("p (c l) -> p c l", c=2)
            dft = C["rat_dft"].rearrange("p (u n) -> p u n", u=U)
            odd = C["rat_odd"].rearrange("p (c n) -> p c n", c=2)
            back = C["rat_back"].rearrange("p (t c u n) -> p t c u n", t=2, c=2, u=U)
            pe.wait_ge(C.sem("base"), C.count("base"))
            pe.wait_ge(C.sem("rat"), C.count("rat"))
            pe.wait_ge(S["nyq"], 7)
            nc.tensor.transpose(banks[4][0:PAIRS, 0:P], nyq[:, 0], ident).then_inc(S["nyq_ps"], 1)
            pe.wait_ge(S["coef"], 1)
            pe.wait_ge(S["nyqT"], 1)
            with pe.Fori(0, ITERS) as it:
                for s in range(RSTEPS):
                    k = s % 2
                    if s >= 2:
                        pe.wait_ge(S["terms"], it * RSTEPS + s - 1)
                        pe.wait_ge(S["sq"], it * RSTEPS + s - 1)
                    cols = bass.ds(it * (RSTEPS * STEP) + s * STEP, STEP)
                    for c in range(2):
                        nc.tensor.matmul(PS[k][:, 0, c * STEP:(c + 1) * STEP], dft9[0:2 * TAPS, c, :], num[:, cols],
                                         start=True, stop=True)
                    for c in range(2):
                        ins = nc.tensor.matmul(PS[k][:, 1, c * STEP:(c + 1) * STEP], dft9[0:TAPS, c, :], den[:, cols],
                                               start=True, stop=True)
                    ins.then_inc(S["coef_ps"], 1)
                    w, half = s // 2, s % 2
                    pe.wait_ge(S["normed"], it * W + w + 1)
                    if s >= 4:
                        pe.wait_ge(S["xf"], it * RSTEPS + s - 3)
                    for u in range(U):
                        ins = nc.tensor.matmul(banks[4 + s % 4], xd[:, w, 2 * u + half].rearrange("p a f -> p (a f)"),
                                               dft[:, u, :], start=(u == 0), stop=(u == U - 1))
                    ins.then_inc(S["xf_ps"], 1)
                pe.wait_ge(S["terms"], it * RSTEPS + RSTEPS)
                pe.wait_ge(S["sq"], it * RSTEPS + RSTEPS)
                pe.wait_ge(S["xf"], it * RSTEPS + RSTEPS)
            pe.wait_ge(S["ht"], STEPS)
            pe.wait_ge(S["ht_row"], 16)
            pe.wait_ge(S["xf"], STEPS)
            for m in range(PAIRS):
                if m >= 8:
                    pe.wait_ge(S["hf_odd"] if m % 2 else S["hf_even"], (m - 8) // 2 + 1)
                bank = banks[m % 8]
                part_of = [ht[:, c, m * P:(m + 1) * P] for c in range(2)]
                for c in range(2):
                    nc.tensor.transpose(bank[:, c * LT:(c + 1) * LT], part_of[c], ident)
                for c in range(2):
                    ins = nc.tensor.matmul(bank[:, 2 * LT:], part_of[c], odd[:, c, :], start=(c == 0), stop=(c == 1))
                ins.then_inc(S["hf_ps"], 1)
            pe.wait_ge(S["hf_even"], PAIRS // 2)
            pe.wait_ge(S["hf_odd"], PAIRS // 2)
            pe.wait_ge(S["ends"], 2)
            for l in range(LT):
                bank = banks[l // 8 % 8]
                if l % 8 == 0 and l >= 64:
                    g = l // 8
                    pe.wait_ge(S["prod_odd"] if g % 2 else S["prod_even"], (g - 8) // 2 + 1)
                cols = slice(l % 8 * D, (l % 8 + 1) * D)
                for tile in range(2):
                    if tile == 0 and l == 0:
                        for x in range(2):
                            nc.tensor.matmul(bank[x * 2 * B:(x + 1) * 2 * B, cols], xf[:, 0, 0, x].rearrange("p j b -> p (j b)"),
                                             ends[:, x].rearrange("p c m -> p (c m)"), start=True, stop=True)
                    else:
                        ins = nc.tensor.matmul(bank[tile * D:(tile + 1) * D, cols],
                                               xf[:, tile, l].rearrange("p x j b -> p (x j b)"),
                                               resp[:, tile, l].rearrange("p c m -> p (c m)"), start=True, stop=True)
                if l % 8 == 7:
                    ins.then_inc(S["prod_ps"], 1)
            pe.wait_ge(S["prod_even"], LT // 16)
            pe.wait_ge(S["prod_odd"], LT // 16)
            for g in range(PAIRS // 2):
                if g >= 4:
                    pe.wait_ge(S["Y"], g - 3)
                for k in range(4):
                    m, c = 2 * g + k // 2, k % 2
                    ins = nc.tensor.transpose(banks[g % 4][:, k * P:(k + 1) * P], prod[:, c * PAIRS + m, :], ident)
                ins.then_inc(S["prodT_ps"], 1)
            for k in range(2 * U):
                u, nh = k // 2, k % 2
                pe.wait_ge(S["Y"], (nh + 1) * PAIRS // 4)
                for t in range(2):
                    for c in range(2):
                        ins = nc.tensor.matmul(banks[4 + k], back[:, t, c, u, :], Y[:, t, c, nh * 512:(nh + 1) * 512],
                                               start=(t + c == 0), stop=(t + c == 2))
                ins.then_inc(S["out_ps"], 1)



TAKEN = T // 2 - 1
HID3 = 4 * D
SLABS = HID3 // P


def depth_ffn(nc, H, PS, C, dram):
    with ExitStack() as ctx:
        S = semaphores(nc, "dep",
                        "h_plus_x wb own wn compared rank taken scale y_ps ys h_new xT_ps xT wb_ps hid0_ps "
                        "hid1_ps hid0 hid1 yT_ps yT")
        sb = lambda name, shape, dt=F32: ctx.enter_context(nc.sbuf_tensor("dep_" + name, shape, dt))
        N = NormBuffers(nc, ctx, "dep")
        xc, xn = sb("xc", [P, W, G4, D]), sb("xn", [P, W, G4, D])
        xT = sb("xT", [P, W, T])
        wb = sb("wb", [P, W, 2 * U, P])
        own = sb("own", [P, W, 2 * U, P])
        wn = sb("wn", [P, W, 2 * U])
        junk = sb("junk", [P, 2, T])
        larger, equal = sb("larger", [P, W, 2 * U]), sb("equal", [P, W, 2 * U])
        scale = sb("scale", [P, W, 2 * U])
        hid = sb("hid", [P, W, SLABS, 2 * T])
        yT = sb("yT", [D, W, 2 * T])
        ys = sb("ys", [P, W, G4, D])
        block = ctx.enter_context(nc.Block())
        hx = lambda it: (lambda w: groups(chunk_of(H, it, w)))

        @block.gpsimd
        def _(pool):
            with pool.Fori(0, ITERS) as it:
                norm_rstd(nc, pool, S, C, N, it)
                for w in range(W):
                    pool.wait_ge(S["normed"], it * W + w + 1)
                    x = hx(it)(w)
                    nc.gpsimd.tensor_tensor(x, x, xn[:, w], ALU.add).then_inc(S["h_plus_x"], 1)

        @block.vector
        def _(v):
            v.wait_ge(C.sem("dep"), C.count("dep"))
            before = C["dep_before"].rearrange("p (u n) -> p u n", u=U)
            with v.Fori(0, ITERS) as it:
                norm_stats(nc, v, S, hx(it), N, it)
                norm_apply(nc, v, S, hx(it), N, xc, xn, it)
                for w in range(W):
                    v.wait_ge(S["wb"], it * W + w + 1)
                    nc.vector.tensor_tensor(own[:, w], wb[:, w], bcast(C["ident"], 1, 2 * U), ALU.mult)\
                        .then_inc(S["own"], 1)
                for w in range(W):
                    v.wait_ge(S["own"], it * W + w + 1)
                    nc.vector.tensor_reduce(wn[:, w], own[:, w], AX, ALU.add).then_inc(S["wn"], 1)
                for w in range(W):
                    v.wait_ge(S["wn"], it * W + w + 1)
                    for half in range(2):
                        for u in range(U):
                            k = half * U + u
                            all_w = wb[:, w, half * U:(half + 1) * U, :].rearrange("p u q -> p (u q)")
                            nc.vector.tensor_scalar(junk[:, 0, :], all_w, wn[:, w, k:k + 1], 0.0, ALU.is_gt, ALU.add,
                                                    accum_out=larger[:, w, k:k + 1])
                            nc.vector.scalar_tensor_tensor(junk[:, 1, :], all_w, wn[:, w, k:k + 1], before[:, u, :],
                                                           ALU.is_equal, ALU.mult,
                                                           accum_out=equal[:, w, k:k + 1]).then_inc(S["compared"], 1)
                            v.wait_ge(S["compared"], it * (4 * W) + 4 * w + k + 1)
                v.wait_ge(S["compared"], it * (4 * W) + 4 * W)
                nc.vector.tensor_tensor(larger[:], larger[:], equal[:], ALU.add).then_inc(S["rank"], 1)
                v.wait_ge(S["rank"], it + 1)
                nc.vector.tensor_scalar(scale[:], larger[:], float(TAKEN), None, ALU.is_lt).then_inc(S["taken"], 1)
                v.wait_ge(S["taken"], it + 1)
                nc.vector.tensor_tensor(scale[:], scale[:], wn[:], ALU.mult).then_inc(S["scale"], 1)
                v.wait_ge(S["scale"], it + 1)
                for w in range(W):
                    v.wait_ge(S["y_ps"], it * W + w + 1)
                    s = bcast(scale[:, w].rearrange("p (h u) -> p u h", h=2), 3, D)
                    g4 = lambda ap: ap.rearrange("p (u h) f -> p u h f", u=U)
                    nc.vector.tensor_tensor(g4(ys[:, w]), g4(groups(PS[w][:, 1, 0:CW])), s, ALU.mult).then_inc(S["ys"], 1)
                for w in range(W):
                    v.wait_ge(S["ys"], it * W + w + 1)
                    v.wait_ge(S["h_plus_x"], it * W + w + 1)
                    x = hx(it)(w)
                    nc.vector.tensor_tensor(x, x, ys[:, w], ALU.add).then_inc(S["h_new"], 1)
                v.wait_ge(S["h_new"], it * W + W)

        @block.scalar
        def _(act):
            act.wait_ge(C.sem("dep"), C.count("dep"))
            with act.Fori(0, ITERS) as it:
                for w in range(W):
                    act.wait_ge(S["xT_ps"], it * W + w + 1)
                    nc.scalar.copy(xT[:, w], PS[w][:, 0, 0:T]).then_inc(S["xT"], 1)
                for w in range(W):
                    act.wait_ge(S["wb_ps"], it * W + w + 1)
                    nc.scalar.activation(wb[:, w].rearrange("p k q -> p (k q)"), PS[w][:, 1, :], ACT.Identity,
                                         bias=C["dep_br"]).then_inc(S["wb"], 1)
                for w in range(W):
                    for s in range(SLABS):
                        act.wait_ge(S["hid0_ps"] if s == 0 else S["hid1_ps"], it * W + w + 1)
                        nc.scalar.activation(hid[:, w, s, :], PS[w][:, s, :], ACT.Gelu_apprx_tanh,
                                             bias=C["dep_b1"][:, s:s + 1]).then_inc(S["hid0"] if s == 0 else S["hid1"], 1)
                for w in range(W):
                    act.wait_ge(S["yT_ps"], it * W + w + 1)
                    nc.scalar.activation(yT[:, w], PS[w][0:D, 0, :], ACT.Identity, bias=C["dep_b2"][0:D, :])\
                        .then_inc(S["yT"], 1)

        @block.tensor
        def _(pe):
            ident = C["ident"]
            w1 = C["dep_w1"].rearrange("p (s h n) -> p s h n", s=SLABS, h=2)
            w2 = C["dep_w2"].rearrange("p (s f) -> p s f", s=SLABS)
            wr = C["dep_wr"].rearrange("p (h n) -> p h n", h=2)
            pe.wait_ge(C.sem("dep"), C.count("dep"))
            with pe.Fori(0, ITERS) as it:
                for w in range(W):
                    pe.wait_ge(S["normed"], it * W + w + 1)
                    for u in range(U):
                        ins = nc.tensor.transpose(PS[w][:, 0, u * P:(u + 1) * P],
                                                  xn[:, w, 2 * u:2 * u + 2, :].rearrange("p g f -> p (g f)"), ident)
                    ins.then_inc(S["xT_ps"], 1)
                for w in range(W):
                    pe.wait_ge(S["xT"], it * W + w + 1)
                    for half in range(2):
                        ins = nc.tensor.matmul(PS[w][:, 1, half * T:(half + 1) * T], wr[:, half, :], xT[:, w],
                                               start=True, stop=True)
                    ins.then_inc(S["wb_ps"], 1)
                for w in range(W):
                    for s in range(SLABS):
                        if s == 1:
                            pe.wait_ge(S["wb"], it * W + w + 1)
                        for half in range(2):
                            ins = nc.tensor.matmul(PS[w][:, s, half * T:(half + 1) * T], w1[:, s, half, :], xT[:, w],
                                                   start=True, stop=True)
                        ins.then_inc(S["hid0_ps"] if s == 0 else S["hid1_ps"], 1)
                for w in range(W):
                    pe.wait_ge(S["hid0"], it * W + w + 1)
                    pe.wait_ge(S["hid1"], it * W + w + 1)
                    for s in range(SLABS):
                        ins = nc.tensor.matmul(PS[w][0:D, 0, :], w2[:, s, :], hid[:, w, s, :], start=(s == 0),
                                               stop=(s == SLABS - 1))
                    ins.then_inc(S["yT_ps"], 1)
                for w in range(W):
                    pe.wait_ge(C.sem("base"), C.count("base"))
                    pe.wait_ge(S["yT"], it * W + w + 1)
                    for g in range(G4):
                        at = (g % 2) * T + (g // 2) * P
                        ins = nc.tensor.transpose(PS[w][:, 1, g * D:(g + 1) * D], yT[:, w, at:at + P],
                                                  ident[0:D, 0:D])
                    ins.then_inc(S["y_ps"], 1)
                pe.wait_ge(S["h_new"], it * W + W)



def lay_out(np, x):
    f32 = np.float32
    x = {k: np.asarray(v) for k, v in x.items()}

    def both(w):
        z = np.zeros((2, D, 2, w.shape[1]), w.dtype)
        z[0, :, 0], z[1, :, 1] = w, w
        return z.reshape(2 * D, 2 * w.shape[1])

    def each(w):
        z = np.zeros((2, D, 2, w.shape[1]), w.dtype)
        z[0, :, 0], z[1, :, 1] = w, w
        return z.reshape(2 * D, 2 * w.shape[1])

    def column(b):
        return np.concatenate([b] * (P // b.shape[0]))[:, None]

    def rows(b):
        return np.repeat(b.reshape(1, -1), P, axis=0)

    groups_ = {}
    c = groups_["base"] = {}
    c["ident"] = np.eye(P, dtype=f32)
    taps = x["L0_tok_W"].transpose(2, 1, 0).reshape(KS * D, D)
    main = taps[:KC * P].reshape(KC, P, D).transpose(1, 0, 2).reshape(P, KC * D)
    c["tok_w"] = np.concatenate([main, np.concatenate([taps[KC * P:], np.zeros((D, D), f32)])], axis=1)
    c["tok_b"] = rows(x["L0_tok_b"])
    c = groups_["early"] = {}
    wq, wk, wv = x["L0_attn_Wq"].T, x["L0_attn_Wkv"][:D].T, x["L0_attn_Wkv"][D:].T
    c["lin_q"], c["lin_k"], c["lin_v"], c["lin_o"] = both(wq), both(wk), both(wv), both(x["L0_attn_Wproj"].T)
    c["lin_b"] = rows(x["L0_attn_bproj"])
    c["lin_mask"] = np.kron(np.eye(P // 8, dtype=f32), np.ones((8, 8), f32))
    c["rff_wi"] = each(x["L0_ffn_Wi"].T)
    c["rff_shared"] = x["L0_ffn_Ws"][:, 0].transpose(2, 0, 1).reshape(P, 2 * P)
    c["rff_wo"] = x["L0_ffn_Wo"].T
    c["rff_bs"] = x["L0_ffn_bs"][:, 0].T
    c["rff_bi"], c["rff_bo"] = column(x["L0_ffn_bi"]), column(x["L0_ffn_bo"])
    for k in "qkvl":
        c["bna_w" + k] = both(x["L1_attn_W" + k])
    eye = np.eye(D, dtype=f32)
    lower, upper = np.kron([[1], [0]], np.tile(eye, 2)), np.kron([[0], [1]], np.tile(eye, 2))
    c["bna_halves"] = np.concatenate([lower, upper, lower + upper], axis=1).astype(f32)
    c["bna_bv"], c["bna_bl"] = rows(x["L1_attn_bv"]), rows(x["L1_attn_bl"])
    c["bna_gamma"], c["bna_beta"] = column(x["L1_attn_gamma"]), column(x["L1_attn_beta"])
    c["bna_bq"], c["bna_bk"] = column(x["L1_attn_bq"]), column(x["L1_attn_bk"])
    c = groups_["gate"] = {}
    c["prio"] = rows(np.arange(E8, 0, -1, dtype=f32))
    order = [u * 2 + half for half in range(2) for u in range(U)]
    c["gmask"] = np.tile(np.kron(np.eye(G4, dtype=f32)[:, order], np.ones((E8, 1), f32)), (PARTS, 1))
    for pre, hid, w1, b1, w2, b2, router, br in (
        ("m1", 128, x["L1_ffn_W1"], x["L1_ffn_b1"], x["L1_ffn_W2"], x["L1_ffn_b2"], x["L1_ffn_Wr"], x["L1_ffn_br"]),
        ("m2", 64, x["L2_ffn_w1"], x["L2_ffn_b1"], x["L2_ffn_w2"], x["L2_ffn_b2"], x["L2_ffn_router_w"].T,
         np.zeros(E8, f32)),
    ):
        c = groups_[pre] = {}
        slabs = E8 * hid // P
        cols = w1.transpose(1, 0, 2).reshape(D, slabs, P)
        c[pre + "_w1"] = np.concatenate([each(cols[:, s]) for s in range(slabs)], axis=1)
        c[pre + "_w2"] = w2.reshape(slabs, P, D).transpose(1, 0, 2).reshape(P, slabs * D)
        c[pre + "_b1"] = b1.reshape(slabs, P).T
        c[pre + "_b2"] = np.tile(b2, (PARTS * G4, 1))
        c[pre + "_router"] = both(router)
        c[pre + "_br"] = rows(br)
        pick = np.kron(np.eye(E8, dtype=f32), np.ones((1, hid), f32))
        c[pre + "_sel"] = np.tile(pick, (PARTS * G4, 1))
    groups_["m1"]["m1_gamma"], groups_["m1"]["m1_beta"] = column(x["L1_ffn_gamma"]), column(x["L1_ffn_beta"])
    c = groups_["win"] = {}
    qkv = np.concatenate([x["L2_attn_W_Q"], x["L2_attn_W_K"], x["L2_attn_W_V"]]).reshape(GROUPS6, D, D)
    c["win_qkv"] = np.concatenate([both(m.T) for m in qkv], axis=1)
    theta = (f32(10000.0) ** (f32(-2.0) * np.arange(ROPE // 2, dtype=f32) / f32(ROPE))).astype(f32)
    angle = np.arange(T, dtype=f32)[:, None] * theta[None, :]
    cos, sin = (np.repeat(fn(angle).astype(f32), 2, axis=1) for fn in (np.cos, np.sin))
    flip = np.tile(np.array([-1, 1], f32), ROPE // 2)

    def tokens(a):
        return np.repeat(a.reshape(U, P, 1, ROPE).transpose(1, 0, 2, 3), GROUPS6, axis=2).reshape(P, -1)

    c["win_cos"], c["win_sin"] = tokens(cos), tokens(sin * flip)
    gains = np.concatenate([x["L2_attn_wq"], x["L2_attn_wk"][None], x["L2_attn_wv"][None]])
    tail = gains[:, PLAIN:]
    c["win_w"] = rows(tail)
    c["win_ws"] = rows(tail.reshape(GROUPS6, ROPE // 2, 2)[:, :, ::-1])
    ones = np.ones((ROPE,), f32)
    c["win_wqT"] = np.tile(np.concatenate([x["L2_attn_wq"].T[:PLAIN], np.ones((ROPE, HEADS), f32)]), (2, 1))
    c["win_wkT"] = np.tile(np.concatenate([x["L2_attn_wk"][:PLAIN], ones])[:, None], (2, 1))
    c["win_wv"] = rows(np.concatenate([x["L2_attn_wv"][:PLAIN], ones]))
    back = [np.ones((PLAIN, T), f32), cos.T, (sin * -flip).T]
    c["win_turn"] = np.concatenate(back)
    q_, k_ = np.arange(BLK)[:, None], np.arange(SPAN)[None, :]
    seen = (k_ > q_) & (k_ <= q_ + WIN)
    mask = np.repeat(np.where(seen, 0, -1e30).astype(f32)[None], BLOCKS, axis=0)
    mask[0, :, :WIN] = -1e30
    c["win_mask"] = np.tile(mask.transpose(1, 0, 2).reshape(BLK, BLOCKS * SPAN), (HEADS, 1))
    heads = []
    for j in range(HEADS):
        part = x[f"L2_attn_Wg{j // 2}"][:, (j % 2) * D:(j % 2 + 1) * D]
        heads.append(np.concatenate([part, part[:, PLAIN:]], axis=1))
    c["win_wg"] = np.concatenate(heads, axis=1)
    wo = x["L2_attn_Wout"].T
    c["win_wo"] = np.concatenate([wo[:D], wo[D:]], axis=1)
    c["win_wo2"] = wo
    c["win_bg"] = np.concatenate([x["L2_attn_bg0"], x["L2_attn_bg1"]])[:, None]
    c["win_bout"] = x["L2_attn_bout"][:, None]
    c = groups_["rat"] = {}
    dt, f64 = 2 * np.pi / (2 * T), np.float64
    slot = np.arange(LT)
    freq = np.stack([2 * slot, 2 * slot + 1])
    time = np.arange(T)
    turn = dt * (time[:, None, None] * freq[None])
    forward = np.stack([np.cos(turn), -np.sin(turn)], axis=2)
    forward[:, 0, 1, 0] = (-1.0) ** time
    inverse = np.stack([np.cos(turn), -np.sin(turn)], axis=2) * (2.0 / (2 * T))
    inverse[:, 0, 0, 0] = 1.0 / (2 * T)
    inverse[:, 0, 1, 0] = (-1.0) ** time / (2 * T)
    c["rat_dft"] = forward.reshape(U, P, -1).transpose(1, 0, 2).reshape(P, -1).astype(f32)
    c["rat_back"] = inverse.reshape(U, P, 2, 2, LT).transpose(4, 2, 3, 0, 1).reshape(P, -1).astype(f32)
    half_inverse = 2 * inverse[:, 0]
    odd = np.einsum("tcl,tdk->lcdk", half_inverse, forward[:, 1])
    c["rat_odd"] = odd.reshape(P, -1).astype(f32)
    taps_ = np.cos(2 * dt * np.arange(TAPS)[:, None] * slot), -np.sin(2 * dt * np.arange(TAPS)[:, None] * slot)
    dft9 = np.concatenate(taps_, axis=1).astype(f32)
    c["rat_dft9"] = np.concatenate([dft9, dft9])
    den = np.concatenate([np.ones((D, D, 1), f32), x["L3_attn_denumerator"]], axis=2)
    num = np.concatenate([np.zeros((D, D, 1), f32), x["L3_attn_numerators"][0]], axis=2)

    def pairs(a):
        return a.reshape(D, PAIRS, 2, -1).transpose(2, 0, 1, 3).reshape(P, -1)

    c["rat_a"], c["rat_b"] = pairs(den), pairs(num)
    c["rat_h0"] = pairs(x["L3_attn_h0"].reshape(D, D, 1))
    c["rat_signs"] = rows((-1.0) ** np.arange(TAPS)).astype(f32)
    c = groups_["dep"] = {}
    c["dep_w1"] = np.concatenate([each(x["L3_ffn_w1"][:, s * P:(s + 1) * P]) for s in range(SLABS)], axis=1)
    c["dep_wr"] = each(np.repeat(x["L3_ffn_wr"], P, axis=1))
    c["dep_w2"] = x["L3_ffn_w2"].reshape(SLABS, P, D).transpose(1, 0, 2).reshape(P, SLABS * D)
    c["dep_b1"] = x["L3_ffn_b1"].reshape(SLABS, P).T
    c["dep_b2"] = x["L3_ffn_b2"][:, None]
    c["dep_br"] = rows(x["L3_ffn_br"])
    token = np.arange(P)[:, None, None] + P * np.arange(U)[None, :, None]
    c["dep_before"] = (np.arange(T)[None, None, :] < token).astype(f32).reshape(P, U * T)
    arrays, layout = {}, {}
    for group, columns in groups_.items():
        at, where = 0, {}
        for name, a in columns.items():
            if a.shape[0] < P:
                a = np.concatenate([a, np.zeros((P - a.shape[0], a.shape[1]), a.dtype)])
            columns[name] = a
            where[name] = (at, a.shape[1])
            at += a.shape[1]
        arrays["w_" + group] = np.ascontiguousarray(np.concatenate(list(columns.values()), axis=1))
        layout[group] = (at, where)
    ids = x["x"].reshape(2, CHUNKS, U, P)
    arrays["ids"] = np.ascontiguousarray(ids.transpose(3, 1, 2, 0).reshape(P, CHUNKS * G4))
    emb = x["L0_tok_emb"]
    arrays["emb"] = np.concatenate([emb[:1]] * (KS // 2) + [emb] + [emb[-1:]] * (KS // 2))
    weights = x["L0_ffn_Wr"].transpose(1, 3, 0, 2).reshape(EXPERTS * P, 2 * HID)
    biases = x["L0_ffn_br"].transpose(1, 2, 0).reshape(EXPERTS * P, 2)
    arrays["routed"] = np.concatenate([weights, biases], axis=1)
    route = x["L0_ffn_route_id"].astype(np.int32).reshape(2, CHUNKS, SEGS // 2)
    arrays["route"] = np.ascontiguousarray(route.transpose(1, 0, 2).reshape(1, -1))
    coef = lambda a: a.transpose(2, 1, 0).reshape(a.shape[2], D * D)
    arrays["rat_den"] = np.ascontiguousarray(coef(den))
    h0 = np.repeat(x["L3_attn_h0"].reshape(D, D, 1), TAPS, axis=2)
    arrays["rat_num"] = np.ascontiguousarray(np.concatenate([coef(h0), coef(num)]))
    return arrays, layout



SLOT = {"m1": 0, "m2": 0, "dep": 0, "early": 1, "win": 1, "rat": 1}
AT_START = ("base", "early", "gate", "m1")


class Packed:

    def __init__(self, nc, ctx, layout, dram):
        self.where, self.dram, self.tensors, self.sems = layout, dram, {}, {}
        for slot in (0, 1):
            width = max(n for g, (n, _) in layout.items() if SLOT.get(g) == slot)
            shared = ctx.enter_context(nc.sbuf_tensor(f"w_slot{slot}", [P, width], F32))
            for group, (n, _) in layout.items():
                if SLOT.get(group) == slot:
                    self.tensors[group] = shared[:, 0:n]
        for group, (width, _) in layout.items():
            if group not in SLOT:
                self.tensors[group] = ctx.enter_context(nc.sbuf_tensor(f"w_{group}", [P, width], F32))[:]
            self.sems[group] = ctx.enter_context(nc.semaphore(f"loaded_{group}"))

    def load(self, sp, group):
        sp.dma_start(self.tensors[group], self.dram["w_" + group]).then_inc(self.sems[group], 16)

    def __getitem__(self, name):
        for group, (_, columns) in self.where.items():
            if name in columns:
                at, width = columns[name]
                return self.tensors[group][:, at:at + width]
        raise KeyError(name)

    def sem(self, group):
        return self.sems[group]

    def count(self, group):
        return 16


def tower(nc, dram, layout, out):
    with ExitStack() as ctx:
        H = ctx.enter_context(nc.sbuf_tensor("H", [P, CHUNKS * CW], F32))
        PS = [ctx.enter_context(nc.psum_tensor(f"PS{w}", [P, 2, 512], F32)) for w in range(W)]
        C = Packed(nc, ctx, layout, dram)
        minus_half = ctx.enter_context(nc.sbuf_tensor("minus_half", [P, W * G4], F32))
        C.minus_half = minus_half
        stored = ctx.enter_context(nc.semaphore("stored"))
        const = ctx.enter_context(nc.semaphore("const"))
        with nc.Block() as block:
            @block.sync
            def _(sp):
                for group in AT_START:
                    C.load(sp, group)

            @block.gpsimd
            def _(pool):
                nc.gpsimd.memset(minus_half[:], -0.5).then_inc(const, 1)
        stages = [
            token_convolution,
            linear_attention,
            routed_ffn,
            batchnorm_attention,
            gelu_moe_128,
            window_attention,
            gelu_moe_64,
            rational_convolution,
            depth_ffn,
        ]
        for stage in stages:
            with nc.cleanup_on_exit():
                stage(nc, H, PS, C, dram)
        with nc.Block() as block:
            @block.sync
            def _(sp):
                ov = out.rearrange("(h c) (u p) f -> u h p c f", h=2, u=U)
                hv = H[:].rearrange("p (c u h f) -> p u h c f", c=CHUNKS, u=U, h=2)
                for u in range(U):
                    for half in range(2):
                        sp.dma_start(ov[u, half], hv[:, u, half]).then_inc(stored, 16)
                sp.wait_ge(stored, 16 * U * 2)



def kernel(**inputs):
    import numpy as np
    import concourse.bacc as bacc
    from concourse.bass_utils import run_bass_kernel_spmd

    arrays, layout = lay_out(np, inputs)
    nc = bacc.Bacc("TRN2", target_bir_lowering=False, num_devices=1)
    dram = {}
    for name, a in arrays.items():
        dram[name] = nc.dram_tensor("in_" + name, a.shape, mybir.dt.from_np(a.dtype), kind="ExternalInput").ap()
    out = nc.dram_tensor("out", (B, T, D), F32, kind="ExternalOutput").ap()
    tower(nc, dram, layout, out)
    result = run_bass_kernel_spmd(nc, [{"in_" + name: a for name, a in arrays.items()}], core_ids=[0])
    return result.results[0]["out"]
```
